# Optimizing a Trainium2 kernel written in Bass

```python
import numpy as np
import jax
import jax.numpy as jnp

def _softmax(x, axis=-1):
    return jax.nn.softmax(x, axis=axis)

def _gelu(x):
    return jax.nn.gelu(x, approximate=True)

def _silu(x):
    return jax.nn.silu(x)

def _sigmoid(x):
    return jax.nn.sigmoid(x)

def _layernorm(x, axis=-1, eps=1e-05):
    m = jnp.mean(x, axis=axis, keepdims=True)
    v = jnp.var(x, axis=axis, keepdims=True)
    return (x - m) / jnp.sqrt(v + eps)

def _scatter_add(tgt, idx, src, axis=0):
    return tgt.at[idx].add(src)

def _segment_sum(src, seg, n):
    return jax.ops.segment_sum(src, seg, n)
kernel_name = 'mk_prb_d2_jaxref_r8_00ef06'

def setup_inputs(seed: int=0):
    np.random.seed(seed)
    _w = jnp.asarray

    def _L0_attn_setup():
        import jax, jax.numpy as jnp
        import numpy as np
        B, T, C = (2, 256, 128)
        H, DK, OUT = (16, 64, 128)
        key = jax.random.key(seed)
        k1, k2, k3, k4, k5 = jax.random.split(key, 5)
        glorot_qkv = (2.0 / (C + H * DK)) ** 0.5
        glorot_o = (2.0 / (H * DK + OUT)) ** 0.5
        return {'x': jax.random.normal(k1, (B, T, C), dtype=jnp.float32), 'query_mat': jax.random.normal(k2, (C, H, DK), dtype=jnp.float32) * glorot_qkv, 'key_mat': jax.random.normal(k3, (C, H, DK), dtype=jnp.float32) * glorot_qkv, 'value_mat': jax.random.normal(k4, (C, H, DK), dtype=jnp.float32) * glorot_qkv, 'linear_m1': jax.random.normal(k5, (H * DK, OUT), dtype=jnp.float32) * glorot_o}
    _L0_attn_in = _L0_attn_setup()

    def _L0_ffn_setup():
        import jax, jax.numpy as jnp
        import numpy as np
        THRESH_FACTOR = 0.7

        def ternary_quantize(w):
            delta = THRESH_FACTOR * jnp.mean(jnp.abs(w))
            return jnp.where(w > delta, 1.0, jnp.where(w < -delta, -1.0, 0.0)).astype(w.dtype)
        key = jax.random.key(seed)
        k1, k2, k3 = jax.random.split(key, 3)
        B, S, D_IN, D_OUT = (8, 512, 128, 128)
        inp = {'input': jax.random.normal(k1, (B, S, D_IN), dtype=jnp.float32), 'weight': jax.random.normal(k2, (D_OUT, D_IN), dtype=jnp.float32) * (1.0 / np.sqrt(D_IN)), 'alpha': jnp.ones((1,), dtype=jnp.float32), 'bias': jax.random.normal(k3, (D_OUT,), dtype=jnp.float32) * (1.0 / np.sqrt(D_IN))}
        return inp
    _L0_ffn_in = _L0_ffn_setup()

    def _L1_attn_setup():
        import jax, jax.numpy as jnp
        import numpy as np
        HEAD_DIM = 64
        N_HEADS = 16
        BASE = 10000.0
        MAX_T = 512

        def _rope_tables():
            inv = 1.0 / BASE ** (np.arange(0, HEAD_DIM, 2, dtype=np.float32) / HEAD_DIM)
            t = np.arange(MAX_T, dtype=np.float32)
            ang = np.outer(t, inv)
            return (jnp.asarray(np.cos(ang)), jnp.asarray(np.sin(ang)))
        _COS, _SIN = _rope_tables()

        def apply_rope(x):
            head0, rest = (x[:, :, :1], x[:, :, 1:])
            B, H, N1, D = rest.shape
            xr = rest.reshape(B, H, N1, D // 2, 2)
            xe, xo = (xr[..., 0], xr[..., 1])
            c = _COS[:N1][None, None, :, :]
            s = _SIN[:N1][None, None, :, :]
            re = xe * c - xo * s
            im = xe * s + xo * c
            rot = jnp.stack([re, im], axis=-1).reshape(B, H, N1, D)
            return jnp.concatenate([head0, rot], axis=2)
        key = jax.random.key(seed)
        ks = jax.random.split(key, 5)
        B, N, DIM = (2, 256, 128)
        HD = N_HEADS * HEAD_DIM
        x = jax.random.normal(ks[0], (B, N, DIM), dtype=jnp.float32)
        wq = jax.random.normal(ks[1], (HD, DIM), dtype=jnp.float32) * 0.02
        wk = jax.random.normal(ks[2], (HD, DIM), dtype=jnp.float32) * 0.02
        wv = jax.random.normal(ks[3], (HD, DIM), dtype=jnp.float32) * 0.02
        wo = jax.random.normal(ks[4], (DIM, HD), dtype=jnp.float32) * 0.02
        return {'x': x, 'wq': wq, 'wk': wk, 'wv': wv, 'wo': wo}
    _L1_attn_in = _L1_attn_setup()

    def _L1_ffn_setup():
        import jax, jax.numpy as jnp
        import numpy as np
        CAPACITY_FACTOR = 1.0

        def _route(token_inputs, Wg, capacity):
            dt = token_inputs.dtype
            logits = jnp.einsum('bnd,de->bne', token_inputs, Wg)
            gates = jax.nn.softmax(logits, axis=-1)
            expert_idx = jnp.argmax(gates, axis=-1)
            mask = jax.nn.one_hot(expert_idx, Wg.shape[1], dtype=dt)
            gate = jnp.sum(gates * mask, axis=-1)
            pos = jnp.cumsum(mask, axis=1) * mask - mask
            keep = mask * (pos < capacity).astype(dt)
            pos_oh = jax.nn.one_hot(pos.astype(jnp.int32), capacity, dtype=dt)
            dispatch = keep[..., None] * pos_oh
            combine = dispatch * gate[:, :, None, None]
            return (dispatch, combine)
        key = jax.random.key(seed)
        k1, k2, k3, k4 = jax.random.split(key, 4)
        B, N, D, E, H = (8, 256, 128, 8, 512)
        return {'token_inputs': jax.random.normal(k1, (B, N, D), dtype=jnp.float32), 'Wg': jax.random.normal(k2, (D, E), dtype=jnp.float32) * 0.02, 'W1': jax.random.normal(k3, (E, D, H), dtype=jnp.float32) * 0.02, 'W2': jax.random.normal(k4, (E, H, D), dtype=jnp.float32) * 0.02}
    _L1_ffn_in = _L1_ffn_setup()
    _d = {'L0_attn_x': _L0_attn_in['x'], 'L0_attn_query_mat': _L0_attn_in['query_mat'], 'L0_attn_key_mat': _L0_attn_in['key_mat'], 'L0_attn_value_mat': _L0_attn_in['value_mat'], 'L0_attn_linear_m1': _L0_attn_in['linear_m1'], 'L0_ffn_weight': _L0_ffn_in['weight'], 'L0_ffn_alpha': _L0_ffn_in['alpha'], 'L0_ffn_bias': _L0_ffn_in['bias'], 'L1_attn_wq': _L1_attn_in['wq'], 'L1_attn_wk': _L1_attn_in['wk'], 'L1_attn_wv': _L1_attn_in['wv'], 'L1_attn_wo': _L1_attn_in['wo'], 'L1_ffn_Wg': _L1_ffn_in['Wg'], 'L1_ffn_W1': _L1_ffn_in['W1'], 'L1_ffn_W2': _L1_ffn_in['W2']}
    _x0 = _d['L0_attn_x']
    _d['L0_attn_x'] = jax.random.normal(jax.random.fold_in(jax.random.key(seed), 1), (8, 256, 128), dtype=_x0.dtype)
    del _x0
    return _d

def reference(L0_attn_x, L0_attn_query_mat, L0_attn_key_mat, L0_attn_value_mat, L0_attn_linear_m1, L0_ffn_weight, L0_ffn_alpha, L0_ffn_bias, L1_attn_wq, L1_attn_wk, L1_attn_wv, L1_attn_wo, L1_ffn_Wg, L1_ffn_W1, L1_ffn_W2):

    def _L0_attn_ref(x, query_mat, key_mat, value_mat, linear_m1):
        import jax, jax.numpy as jnp
        import numpy as np
        B, T, C = (2, 256, 128)
        H, DK, OUT = (16, 64, 128)
        q = jnp.einsum('btc,chd->bhtd', x, query_mat)
        k = jnp.einsum('btc,chd->bhtd', x, key_mat)
        v = jnp.einsum('btc,chd->bhtd', x, value_mat)
        d_k = query_mat.shape[-1]
        w = jnp.einsum('bhtd,bhzd->bhtz', q, k) * d_k ** 0.5
        t = w.shape[-1]
        causal = jnp.tril(jnp.ones((t, t), dtype=bool))
        w = jnp.where(causal, w, -jnp.inf)
        w = jax.nn.softmax(w, axis=-1)
        o = jnp.einsum('bhtz,bhzd->bhtd', w, v)
        o = o.transpose(0, 2, 1, 3).reshape(o.shape[0], o.shape[2], -1)
        return jnp.einsum('btc,cz->btz', o, linear_m1)

    def _L0_ffn_ref(input, weight, alpha, bias):
        import jax, jax.numpy as jnp
        import numpy as np
        THRESH_FACTOR = 0.7

        def ternary_quantize(w):
            delta = THRESH_FACTOR * jnp.mean(jnp.abs(w))
            return jnp.where(w > delta, 1.0, jnp.where(w < -delta, -1.0, 0.0)).astype(w.dtype)
        w_ternary = ternary_quantize(weight)
        w_eff = w_ternary * alpha
        out = jnp.einsum('bsd,od->bso', input, w_eff) + bias
        return out

    def _L1_attn_ref(x, wq, wk, wv, wo):
        import jax, jax.numpy as jnp
        import numpy as np
        HEAD_DIM = 64
        N_HEADS = 16
        BASE = 10000.0
        MAX_T = 512

        def _rope_tables():
            inv = 1.0 / BASE ** (np.arange(0, HEAD_DIM, 2, dtype=np.float32) / HEAD_DIM)
            t = np.arange(MAX_T, dtype=np.float32)
            ang = np.outer(t, inv)
            return (jnp.asarray(np.cos(ang)), jnp.asarray(np.sin(ang)))
        _COS, _SIN = _rope_tables()

        def apply_rope(x):
            head0, rest = (x[:, :, :1], x[:, :, 1:])
            B, H, N1, D = rest.shape
            xr = rest.reshape(B, H, N1, D // 2, 2)
            xe, xo = (xr[..., 0], xr[..., 1])
            c = _COS[:N1][None, None, :, :]
            s = _SIN[:N1][None, None, :, :]
            re = xe * c - xo * s
            im = xe * s + xo * c
            rot = jnp.stack([re, im], axis=-1).reshape(B, H, N1, D)
            return jnp.concatenate([head0, rot], axis=2)
        B, N, DIM = x.shape
        scale = HEAD_DIM ** 0.5
        q = x @ wq.T
        k = x @ wk.T
        v = x @ wv.T
        q = q.reshape(B, N_HEADS, N, HEAD_DIM)
        k = k.reshape(B, N_HEADS, N, HEAD_DIM)
        v = v.reshape(B, N_HEADS, N, HEAD_DIM)
        q = apply_rope(q)
        k = apply_rope(k)
        scores = jnp.einsum('bhnd,bhmd->bhnm', q, k) / scale
        w = jax.nn.softmax(scores, axis=-1)
        out = jnp.einsum('bhnm,bhmd->bhnd', w, v)
        out = out.reshape(B, N, N_HEADS * HEAD_DIM)
        return out @ wo.T

    def _L1_ffn_ref(token_inputs, Wg, W1, W2):
        import jax, jax.numpy as jnp
        import numpy as np
        CAPACITY_FACTOR = 1.0

        def _route(token_inputs, Wg, capacity):
            dt = token_inputs.dtype
            logits = jnp.einsum('bnd,de->bne', token_inputs, Wg)
            gates = jax.nn.softmax(logits, axis=-1)
            expert_idx = jnp.argmax(gates, axis=-1)
            mask = jax.nn.one_hot(expert_idx, Wg.shape[1], dtype=dt)
            gate = jnp.sum(gates * mask, axis=-1)
            pos = jnp.cumsum(mask, axis=1) * mask - mask
            keep = mask * (pos < capacity).astype(dt)
            pos_oh = jax.nn.one_hot(pos.astype(jnp.int32), capacity, dtype=dt)
            dispatch = keep[..., None] * pos_oh
            combine = dispatch * gate[:, :, None, None]
            return (dispatch, combine)
        B, N, D = token_inputs.shape
        E = Wg.shape[1]
        capacity = int(N * CAPACITY_FACTOR // E)
        dispatch, combine = _route(token_inputs, Wg, capacity)
        expert_inputs = jnp.einsum('bnd,bnec->becd', token_inputs, dispatch)
        h = jax.nn.gelu(jnp.einsum('becd,edh->bech', expert_inputs, W1))
        expert_outputs = jnp.einsum('bech,ehd->becd', h, W2)
        output = jnp.einsum('becd,bnec->bnd', expert_outputs, combine)
        return output
    x = L0_attn_x
    xn = _layernorm(x, axis=-1)
    x = x + _L0_attn_ref(xn, L0_attn_query_mat, L0_attn_key_mat, L0_attn_value_mat, L0_attn_linear_m1) + _L0_ffn_ref(xn, L0_ffn_weight, L0_ffn_alpha, L0_ffn_bias)
    xn = _layernorm(x, axis=-1)
    x = x + _L1_attn_ref(xn, L1_attn_wq, L1_attn_wk, L1_attn_wv, L1_attn_wo) + _L1_ffn_ref(xn, L1_ffn_Wg, L1_ffn_W1, L1_ffn_W2)
    return x

_drawn_inputs = setup_inputs


def setup_inputs(seed=0):
    import zlib

    import numpy as np

    out = dict(_drawn_inputs(seed))
    spreads = {}
    factors = {'L0_ffn_bias': 5.734,
     'L1_attn_wq': 8.0,
     'L1_attn_wk': 8.0,
     'L1_attn_wv': 8.0,
     'L1_attn_wo': 8.0,
     'L1_ffn_Wg': 8.0,
     'L1_ffn_W1': 8.0,
     'L1_ffn_W2': 8.0}
    for name, (base, spread) in spreads.items():
        noise = np.random.default_rng([zlib.crc32(name.encode()), seed]).standard_normal(out[name].shape)
        drawn = base * np.exp(spread * noise) if base else spread * noise
        out[name] = jnp.asarray(drawn.astype(out[name].dtype))
    for name, factor in factors.items():
        out[name] = (out[name] * factor).astype(out[name].dtype)
    return out
```

```python
from contextlib import ExitStack

import numpy as np

import concourse.bass as bass
from concourse import mybir

P = 128
B, T, C = 8, 256, 128
H, DK = 16, 64
HD = H * DK
NT = T // P
NJ = H // 2
TPH = T // H
E, FF, CAP = 8, 512, T // 8
NF = FF // P
EPS = 1e-5
N_CONST = 8
THRESH = 0.7
NEG = -1.0e30
BIG = 3.0e38

F32 = mybir.dt.float32
F32R = mybir.dt.float32r
ALU = mybir.AluOpType
ACT = mybir.ActivationFunctionType
AX = mybir.AxisListType

NS, NP_, NPT = 3, 3, 2

ROUTE_MASK = 10

PRO, FIRST, FULL, NO_NEXT, LAST = range(5)
I_LOOP, I_NO_NEXT, I_LAST = 1, B - 1, B

QKV1 = [(0, "v1", 0), (0.5, "v1", 1), (1, "v1", 2), (1.5, "v1", 3), (2, "vT", 0), (2.5, "vT", 1), (3, "vT", 2),
        (3.5, "vT", 3), (4, "k1", 0), (4.5, "q1", 0), (5, "k1", 1), (5.5, "q1", 1), (6, "q1", 2), (7, "q1", 3),
        (7.5, "kT", 0), (8, "kT", 1), (8.5, "kT", 2), (9, "kT", 3), (9.5, "k1", 2), (10, "q1", 4), (10.5, "k1", 3),
        (11, "q1", 5), (12, "q1", 6), (13, "kT", 4), (13.5, "kT", 5), (14, "kT", 6), (14.5, "kT", 7), (15, "q1", 7)]
A_TASKS = [(H - 5, "stat", 0), (H - 4, "norm", 0), (H + 4, "proj0", 0), (H + 5, "stat", 1), (H + 6, "norm", 1),
           (H + 8, "xT1", 0), (H + 9.5, "logit", 0), (H + 6, "xT0", 0)]
QKV0 = [(27, "q0", 0), (28, "k0", 0), (29, "q0", 1), (30, "k0", 1), (31, "q0", 2), (32, "k0", 2), (32.5, "q0", 3),
        (33, "k0", 3), (33.5, "v0", 0), (34, "v0", 1), (34.5, "v0", 2), (35, "v0", 3)]


def schedule(kind):
    a = H if kind in (FIRST, FULL, NO_NEXT) else 0
    b = H if kind in (FULL, NO_NEXT, LAST) else 0
    n = a + b
    tasks = []
    if kind == PRO:
        tasks += [(0, "stat", 0), (0, "norm", 0), (0, "xT0", 0)] + [(0, *t[1:]) for t in QKV0]
    if kind == LAST:
        tasks += [(-1, *t[1:]) for t in QKV1]
    if kind in (FULL, NO_NEXT):
        tasks += QKV1
    if a:
        tasks += [t for t in A_TASKS if kind != NO_NEXT or t[1:] not in (("stat", 0), ("norm", 0), ("xT0", 0))]
    if kind == FIRST:
        tasks += [(H + 6, *t[1:]) for t in QKV0]
    if kind == FULL:
        tasks += QKV0
    if b:
        tasks.append((n + 3.5, "proj1", 0))
    out = []
    for s in range(int(min(0, tasks[0][0])), int(max([t[0] for t in tasks] + [n + 3 if n else 0])) + 1):
        if 0 <= s < n:
            out.append(("S", s))
        if 0 <= s - 1 < n:
            out.append(("R", s - 1))
        out += [t[1:] for t in tasks if t[0] == s]
        if 0 <= s - 2 < n:
            out.append(("T", s - 2))
        if 0 <= s - 3 < n:
            out.append(("PV", s - 3))
            if (s - 3) % 2:
                out.append(("O", (s - 3) // 2))
        out += [t[1:] for t in tasks if t[0] == s + 0.5]
    assert all(t[1:] in out for t in tasks)
    done, placed = [0, 0], []
    for what, m in out:
        if what in TASKS:
            bank = sum(done) % 2
            done[bank] += 1
            placed.append((what, m, bank, done[bank]))
        else:
            placed.append((what, m, None, None))
    return placed


TASKS = ("xT0", "q0", "k0", "v0", "proj0", "xT1", "logit", "q1", "k1", "kT", "v1", "vT", "proj1")


def tasks_in(kind, bank):
    return sum(1 for x in schedule(kind) if x[2] == bank)


def task_base(i, bank):
    if isinstance(i, int) and i < 1:
        return 0 if i == -1 else tasks_in(PRO, bank)
    before = tasks_in(PRO, bank) + tasks_in(FIRST, bank)
    if isinstance(i, int) and i == I_LAST:
        return before + (I_NO_NEXT - 1) * tasks_in(FULL, bank) + tasks_in(NO_NEXT, bank)
    return (i - 1) * tasks_in(FULL, bank) + before


def head_base(i):
    return 0 if isinstance(i, int) and i < 1 else i * (2 * H) - H


def pair_base(i):
    return 0 if isinstance(i, int) and i < 1 else i * H - NJ


def batch_rows(i):
    return i * NT


def heads_a(kind):
    return 0 if kind in (PRO, LAST) else H


def task_at(kind, name, m):
    for what, n, bank, place in schedule(kind):
        if (what, n) == (name, m):
            return bank, place
    raise ValueError((kind, name, m))


def build(nc, t_in, out):
    ctx = ExitStack()
    with ctx:
        def sb(name, shape, dt=F32):
            return ctx.enter_context(nc.sbuf_tensor(name, shape, dt))

        def sem(name):
            return ctx.enter_context(nc.semaphore(name))

        w0 = sb("w0", [P, 2, 3, HD], F32R)
        wq1 = sb("wq1", [P, 2, 2 * HD], F32R)
        wkv1 = sb("wkv1", [P, 2, 2, HD], F32R)
        we = sb("we", [P, 2, C], F32R)
        wg = sb("wg", [P, 2, E], F32R)
        lin = sb("lin", [P, NJ, C])
        wo = sb("wo", [P, NJ, C])
        mem0 = sb("mem0", [P, 4096 + 2048 + 3072])
        q_pad = mem0[:, 0:4096].rearrange("p (j a t) -> p j a t", j=NJ, a=2)
        k_pair = mem0[:, 4096:6144].rearrange("p (j t) -> p j t", j=NJ)
        v_pair = mem0[:, 6144:9216].rearrange("p (b j a d) -> p b j a d", b=NT, j=NJ, a=3)
        w1_sb = mem0[:, 0:4096].rearrange("p (e f) -> p e f", e=E)
        w2_sb = mem0[:, 4096:8192].rearrange("p (e f d) -> p e f d", e=E, f=NF)
        q_rot = sb("q_rot", [P, H, 2, NJ, TPH])
        k_dup = sb("k_dup", [P, H, 2, NJ, TPH])
        q_flat = q_rot[:, :, :, :, :].rearrange("p h a j t -> p (h a j t)")
        k_flat = k_dup[:, :, :, :, :].rearrange("p h a j t -> p (h a j t)")
        v_row = sb("v_row", [P, 64 + 2 * H * P])
        v_col = sb("v_col", [P, H, P])
        k_tok = sb("k_tok", [P, NT, H // 2, 2, DK])
        k_cos = v_col[:, 0:4, :].rearrange("p a b -> p (a b)")
        k_sin = v_col[:, 4:8, :].rearrange("p a b -> p (a b)")
        x_all = sb("x_all", [P, B * NT, C])
        lg_all = sb("lg_all", [P, B * NT, E])
        xn0 = sb("xn0", [P, NT, C])
        xn1 = sb("xn1", [P, NT, C])
        xT0 = sb("xT0", [P, 2, T], F32R)
        xT1 = sb("xT1", [P, 2, T], F32R)
        prob = sb("prob", [P, NP_, 512])
        probT = sb("probT", [P, NPT, 512])
        oT = sb("oT", [P, NJ, T])
        nmax = sb("nmax", [P, NS, 2])
        rsum = sb("rsum", [P, NS, 2])
        rinv = sb("rinv", [P, NS, 2])
        stats = sb("stats", [P, 2, NT, 6])
        mv = sb("mv", [P, 2, NT, 2])
        vareps = sb("vareps", [P, 2, NT])
        rstd = sb("rstd", [P, 2, NT])
        ident = sb("ident", [P, P])
        mask = sb("mask", [P, T])
        rope_q = sb("rope_q", [P, NJ, 2, TPH])
        cos_k = sb("cos_k", [P, HD // 2])
        sin_k = sb("sin_k", [P, HD // 2])
        bias = sb("bias", [P, C])
        alpha = sb("alpha", [P, 1])
        ones = sb("ones", [P, P])
        half_pow = sb("half_pow", [P, NT])
        thr = sb("thr", [P, 4])

        ps_s = [ctx.enter_context(nc.psum_tensor(f"ps_s{n}", [P, 512], F32)) for n in range(NS)]
        ps_t = [ctx.enter_context(nc.psum_tensor(f"ps_t{n}", [P, 512], F32)) for n in range(NPT)]
        ps_o = ctx.enter_context(nc.psum_tensor("ps_o", [P, 512], F32))
        ps_m = [ctx.enter_context(nc.psum_tensor(f"ps_m{n}", [P, 512], F32)) for n in range(2)]

        xn_dram = nc.dram_tensor("xn_dram", (B, P, NT * C), F32)

        x_loaded = sem("x_loaded")
        w0_loaded = sem("w0_loaded")
        w1_loaded = sem("w1_loaded")
        wf_loaded = sem("wf_loaded")
        const_loaded = sem("const_loaded")
        experts_loaded = sem("experts_loaded")
        zeroed = sem("zeroed")
        w0_hi, w0_split = sem("w0_hi"), sem("w0_split")
        w1_hi, w1_split = sem("w1_hi"), sem("w1_split")
        thr_step, abs_sum, wf_split = sem("thr_step"), sem("abs_sum"), sem("wf_split")
        s_ready = sem("s_ready")
        max_ready = sem("max_ready")
        p_ready = sem("p_ready")
        rinv_ready = sem("rinv_ready")
        norm_ready = sem("norm_ready")
        t_ready = sem("t_ready")
        t_copied = [sem(f"t_copied{n}") for n in range(2)]
        pv_done = sem("pv_done")
        o_copied = sem("o_copied")
        m_ready = [sem(f"m_ready{n}") for n in range(2)]
        m_done = [sem(f"m_done{n}") for n in range(2)]
        xt_hi = [sem(f"xt_hi{n}") for n in range(2)]
        k_rot = sem("k_rot")
        x1_step = sem("x1_step")
        ln_stat, ln_mv, ln_eps, ln_rstd, xn_ready = [[sem(f"{what}{n}") for n in range(2)] for what in (
            "ln_stat", "ln_mv", "ln_eps", "ln_rstd", "xn_ready")]
        xn_saved = sem("xn_saved")
        passed = sem("passed")
        xn_loaded = sem("xn_loaded")
        route = sem("route")
        route_exp = sem("route_exp")
        pos_ready = sem("pos_ready")
        disp_ready = sem("disp_ready")
        xe_ready, xe_copied = sem("xe_ready"), sem("xe_copied")
        dT_ready, dT_copied = sem("dT_ready"), sem("dT_copied")
        h_ready, h_gelu = sem("h_ready"), sem("h_gelu")
        y_ready, y_copied = sem("y_ready"), sem("y_copied")
        ys_ready, ys_copied = sem("ys_ready"), sem("ys_copied")
        c_ready, out_ready = sem("c_ready"), sem("out_ready")
        out_stored = sem("out_stored")

        xn_all = v_col
        disp = q_flat.rearrange("p (n s) -> p n s", n=B * NT)
        xe = k_flat[:, 0:E * B * CAP].rearrange("p (e b s) -> p e b s", e=E, b=B)
        yT = k_flat[:, E * B * CAP:2 * E * B * CAP].rearrange("p (b e s) -> p b e s", b=B, e=E)
        dT = v_row[:, 0:B * 2 * T].rearrange("p (b f) -> p b f", b=B)
        ys = oT[:, :, :].rearrange("p j t -> p (j t)").rearrange("p (b g d) -> p b g d", b=B, g=2)
        ps_y = [ps_o, ps_t[0]]
        hid = [prob[:, 0:2, :].rearrange("p a f -> p (a f)"), probT[:, :, :].rearrange("p a f -> p (a f)")]
        upper = mem0[:, 8192:8320]
        iota = mem0[:, 8320:8576]
        first_slot = mem0[:, 8576:8704].rearrange("p (n e) -> p n e", e=E)
        rank = mem0[:, 8704:8832].rearrange("p (n e) -> p n e", e=E)
        wide = [x[:, n * 128:(n + 1) * 128].rearrange("p (n e) -> p n e", e=E) for x in (sin_k, cos_k) for n in range(4)]
        thin = [mask[:, n * 16:(n + 1) * 16] for n in range(10)]

        block = ctx.enter_context(nc.Block())

        def wait_apart(eng, s, value):
            eng.wait_ge(s, value)
            if not isinstance(value, int):
                eng.sem_inc(passed, 1)

        def ln_number(block_no, i):
            return i if block_no else i + 1

        @block.sync
        def _(sp):
            xv = t_in["x"].rearrange("b (t p) c -> p (b t) c", p=P)
            sp.dma_start(x_all[:, 0:NT, :], xv[:, 0:NT, :]).then_inc(x_loaded, 16)
            sp.dma_start(ident[:, :], t_in["ident"]).then_inc(const_loaded, 16)
            sp.dma_start(q_flat[:, 0:3 * HD], t_in["w0"]).then_inc(w0_loaded, 16)
            sp.dma_start(mask[:, :], t_in["mask"]).then_inc(const_loaded, 16)
            sp.dma_start(x_all[:, NT:, :], xv[:, NT:, :]).then_inc(x_loaded, 16)
            sp.dma_start(prob[:, 0, 0:C], t_in["wf"]).then_inc(wf_loaded, 16)
            sp.dma_start(prob[:, 0, C:C + E], t_in["wg"]).then_inc(wf_loaded, 16)
            sp.dma_start(alpha[:, :], t_in["alpha"]).then_inc(wf_loaded, 16)
            sp.dma_start(bias[:, :], t_in["bias"]).then_inc(const_loaded, 16)
            sp.dma_start(lin[:, :, :], t_in["lin"].rearrange("(j p) z -> p j z", p=P)).then_inc(const_loaded, 16)
            sp.dma_start(k_flat, t_in["w1"]).then_inc(w1_loaded, 16)
            sp.dma_start(wo[:, :, :], t_in["wo"].rearrange("(j p) z -> p j z", p=P)).then_inc(const_loaded, 16)
            sp.dma_start(rope_q[:, :, :, :].rearrange("p j a t -> p (j a t)"), t_in["rope_q"]).then_inc(const_loaded, 16)
            sp.dma_start(cos_k[:, :], t_in["cos_k"]).then_inc(const_loaded, 16)
            sp.dma_start(sin_k[:, :], t_in["sin_k"]).then_inc(const_loaded, 16)
            with sp.Fori(0, B) as i:
                sp.wait_ge(xn_ready[1], i + 1)
                sp.dma_start(xn_dram[bass.ds(i, 1), :, :].rearrange("b p f -> p (b f)"),
                             xn1[:, :, :].rearrange("p t c -> p (t c)")).then_inc(xn_saved, 16)
            sp.wait_ge(xn_saved, 16 * B)

            sp.wait_ge(pv_done, head_base(I_NO_NEXT) + H)
            sp.wait_ge(s_ready, head_base(I_NO_NEXT) + H)
            sp.dma_start(w1_sb, t_in["We1"].rearrange("e d f -> d e f")).then_inc(experts_loaded, 16)
            for e in range(E):
                sp.dma_start(w2_sb[:, e, :, :], t_in["We2"][e].rearrange("(f p) d -> p f d", p=P)).then_inc(experts_loaded, 16)
            sp.dma_start(mem0[:, 8192:8832], t_in["routing"]).then_inc(experts_loaded, 16)
            sp.wait_ge(k_rot, 4 * B)
            sp.dma_start(xn_all[:, :, :].rearrange("p (b t) c -> p b (t c)", b=B),
                         xn_dram[:, :, :].rearrange("b p f -> p b f")).then_inc(xn_loaded, 16)
            ov = out.rearrange("b (t p) c -> p (b t) c", p=P)
            for b in range(B):
                sp.wait_ge(out_ready, b + 1)
                sp.dma_start(ov[:, b * NT:(b + 1) * NT, :], x_all[:, b * NT:(b + 1) * NT, :]).then_inc(out_stored, 16)
            sp.wait_ge(out_stored, 16 * B)

        @block.tensor
        def _(pe):
            def three(o, wh, wl, xh, xl, start=True, stop=True):
                pe.matmul(o, wh, xh, start=start, stop=False)
                pe.matmul(o, wh, xl, start=False, stop=False)
                return pe.matmul(o, wl, xh, start=False, stop=stop)

            def landed(kind, i, tasks, bank=None, place=0):
                most = {bank: place} if bank is not None else {}
                for name, n in tasks:
                    b, p = task_at(kind, name, n)
                    most[b] = max(most.get(b, 0), p)
                for b, p in sorted(most.items()):
                    if p or not (isinstance(i, int) and i == -1):
                        pe.wait_ge(m_done[b], task_base(i, b) + p)

            def task(kind, i, what, m, bank, place):
                o = ps_m[bank]
                reads = {("q0", 0): [("xT0", 0)], ("k0", 0): [("xT0", 0)], ("logit", 0): [("xT1", 0)],
                         ("vT", 0): [("v1", n) for n in range(4)]}.get((what, m), [])
                landed(kind, i, reads, bank, place - 1)
                if what == "xT0" or what == "xT1":
                    n = int(what == "xT1")
                    pe.wait_ge(xn_ready[n], ln_number(n, i) + 1)
                    src = xn1 if n else xn0
                    for t in range(NT):
                        last = pe.transpose(o[:, t * P:(t + 1) * P], src[:, t, :], ident[:, :])
                elif what in ("q0", "k0"):
                    w = 0 if what == "q0" else 1
                    for a in range(2):
                        col = slice((2 * m + a) * P, (2 * m + a + 1) * P)
                        last = three(o[:, a * T:(a + 1) * T], w0[:, 0, w, col], w0[:, 1, w, col],
                                     xT0[:, 0, :], xT0[:, 1, :])
                elif what == "v0":
                    t, f = m // 2, m % 2
                    tok, col = slice(t * P, (t + 1) * P), slice(f * 512, (f + 1) * 512)
                    last = three(o[:, :], xT0[:, 0, tok], xT0[:, 1, tok], w0[:, 0, 2, col], w0[:, 1, 2, col])
                elif what == "q1":
                    for a in range(2):
                        col = slice((2 * m + a) * P, (2 * m + a + 1) * P)
                        last = three(o[:, a * T:(a + 1) * T], wq1[:, 0, col], wq1[:, 1, col],
                                     xT1[:, 0, :], xT1[:, 1, :])
                elif what == "k1":
                    f, t = m // 2, m % 2
                    tok, col = slice(t * P, (t + 1) * P), slice(f * 512, (f + 1) * 512)
                    last = three(o[:, :], xT1[:, 0, tok], xT1[:, 1, tok], wkv1[:, 0, 0, col], wkv1[:, 1, 0, col])
                elif what == "v1":
                    for a in range(2):
                        col = slice((2 * m + a) * P, (2 * m + a + 1) * P)
                        last = three(o[:, a * T:(a + 1) * T], wkv1[:, 0, 1, col], wkv1[:, 1, 1, col],
                                     xT1[:, 0, :], xT1[:, 1, :])
                elif what == "kT":
                    pe.wait_ge(k_rot, (i - 1) * 4 + 2 * (m // 4) + 2)
                    for a in range(2):
                        c = (2 * m + a) % 8
                        for t in range(NT):
                            src = k_tok[:, t, c, :, :].rearrange("p a d -> p (a d)")
                            last = pe.transpose(o[:, a * T + t * P:a * T + (t + 1) * P], src, ident[:, :])
                elif what == "vT":
                    for a in range(4):
                        last = pe.transpose(o[:, a * P:(a + 1) * P], v_col[:, 4 * m + a, :], ident[:, :])
                elif what == "proj0" or what == "proj1":
                    n_pairs = NJ if what == "proj0" or kind == LAST else 2 * NJ
                    pe.wait_ge(o_copied, pair_base(i) + n_pairs)
                    w = lin if what == "proj0" else wo
                    for t in range(NT):
                        tok = slice(t * P, (t + 1) * P)
                        for j in range(NJ):
                            last = pe.matmul(o[:, tok], oT[:, j, tok], w[:, j, :], start=(j == 0),
                                             stop=(what == "proj1" and j == NJ - 1))
                        if what == "proj0":
                            last = three(o[:, tok], xT0[:, 0, tok], xT0[:, 1, tok], we[:, 0, :], we[:, 1, :],
                                         start=False)
                elif what == "logit":
                    for t in range(NT):
                        tok = slice(t * P, (t + 1) * P)
                        last = three(o[:, t * E:(t + 1) * E], xT1[:, 0, tok], xT1[:, 1, tok],
                                     wg[:, 0, :], wg[:, 1, :])
                last.then_inc(m_ready[bank], 1)

            def scores(kind, i, k):
                o = ps_s[k % NS]
                a = heads_a(kind)
                if k >= NS:
                    pe.wait_ge(p_ready, head_base(i) + k - NS + 1)
                if k < a:
                    j, hh = k // 2, k % 2
                    if k == 0:
                        last_bank = [x for x in schedule(FIRST if kind == FIRST else FULL) if x[2] is not None][-1][2]
                        for n in range(2):
                            pe.wait_ge(m_done[n], task_base(i, n) - int(kind != FIRST and n == last_bank))
                    pe.matmul(o[:, 0:P], q_pad[:, j, hh, 0:P], k_pair[:, j, 0:P], start=True, stop=True)
                    last = pe.matmul(o[:, P:P + T], q_pad[:, j, hh, P:T], k_pair[:, j, :], start=True, stop=True)
                else:
                    h = k - a
                    if h == 0:
                        landed(kind, i, [t[1:] for t in QKV1 if t[1] in ("q1", "kT", "vT")])
                    for e in range(2):
                        last = pe.matmul(o[:, e * T:(e + 1) * T], q_rot[:, h, e, :, :].rearrange("p j t -> p (j t)"),
                                         k_dup[:, h, :, :, :].rearrange("p a j t -> p (a j t)"), start=True, stop=True)
                last.then_inc(s_ready, 1)

            def transposes(kind, i, k):
                o, src = ps_t[k % NPT], prob[:, k % NP_, :]
                pe.wait_ge(norm_ready, head_base(i) + k + 1)
                if k >= NPT:
                    pe.wait_ge(t_copied[k % 2], pair_base(i) + k // 2)
                if k < heads_a(kind):
                    blocks = [(0, 0), (1, 1), (2, 2)]
                else:
                    blocks = [(0, 0), (1, 2), (2, 1), (3, 3)]
                for dst, s in blocks:
                    last = pe.transpose(o[:, dst * P:(dst + 1) * P], src[:, s * P:(s + 1) * P], ident[:, :])
                last.then_inc(t_ready, 1)

            def outputs(kind, i, k):
                a = heads_a(kind)
                pt = probT[:, k % NPT, :]
                pe.wait_ge(t_copied[k % 2], pair_base(i) + k // 2 + 1)
                pair = k // 2
                if k % 2 == 0 and pair >= 1:
                    pe.wait_ge(o_copied, pair_base(i) + pair)
                o = ps_o[:, 0:T]
                if k < a:
                    j, hh = k // 2, k % 2
                    pe.matmul(o, v_pair[:, 0, j, hh:hh + 2, :].rearrange("p a d -> p (a d)"), pt[:, 0:T],
                              start=(hh == 0), stop=False)
                    last = pe.matmul(o[:, P:T], v_pair[:, 1, j, hh:hh + 2, :].rearrange("p a d -> p (a d)"), pt[:, T:384],
                                     start=False, stop=(hh == 1))
                else:
                    h = k - a
                    oh = o[:, (k % 2) * P:(k % 2 + 1) * P]
                    for kb in range(2):
                        at = P * (2 * h + kb)
                        for e in range(2):
                            w = v_row[:, at + 64:at + 64 + P] if e == 0 else v_row[:, at:at + P]
                            last = pe.matmul(oh, w, pt[:, (2 * kb + e) * P:(2 * kb + e + 1) * P],
                                             start=(kb == 0 and e == 0), stop=(kb == 1 and e == 1))
                last.then_inc(pv_done, 1)

            def iteration(kind, i):
                for what, m, bank, place in schedule(kind):
                    if what == "S":
                        scores(kind, i, m)
                    elif what == "T":
                        transposes(kind, i, m)
                    elif what == "PV":
                        outputs(kind, i, m)
                    elif bank is not None:
                        if kind == LAST and place == 1:
                            landed(kind, i, [], 1 - bank, 0)
                        task(kind, i, what, m, bank, place)

            pe.wait_ge(const_loaded, 16 * N_CONST)
            pe.wait_ge(zeroed, 3)
            pe.wait_ge(thr_step, 1)
            pe.matmul(ps_t[0][:, 0:1], ones[:, :], thr[:, 0:1], start=True, stop=True).then_inc(abs_sum, 1)
            pe.wait_ge(w0_split, 1)
            iteration(PRO, -1)
            pe.wait_ge(wf_split, 2)
            iteration(FIRST, 0)
            pe.wait_ge(w1_split, 1)
            with pe.Fori(I_LOOP, I_NO_NEXT) as i:
                iteration(FULL, i)
            iteration(NO_NEXT, I_NO_NEXT)
            iteration(LAST, I_LAST)

            pe.wait_ge(experts_loaded, 16 * (E + 2))
            pe.wait_ge(route, ROUTE_MASK)
            chosen = wide[5].rearrange("p (b t) e -> p b t e", t=NT)
            pe.matmul(ps_s[0][:, 0:B * E], upper, chosen[:, :, 0, :], start=True, stop=True)
            pe.matmul(ps_s[0][:, B * E:2 * B * E], upper, chosen[:, :, 1, :], start=True, stop=False)
            pe.matmul(ps_s[0][:, B * E:2 * B * E], ones[:, :], chosen[:, :, 0, :], start=False, stop=True).then_inc(pos_ready, 1)
            pe.wait_ge(xn_loaded, 16)
            for n in range(2):
                pe.wait_ge(t_copied[n], pair_base(I_LAST) + NJ)
                pe.wait_ge(m_done[n], task_base(I_LAST, n) + tasks_in(LAST, n))
            for b in range(B):
                pe.wait_ge(disp_ready, NT * (b + 1))
                bank = ps_t[b // 2 % 2]
                if b % 2 == 0 and b >= 4:
                    pe.wait_ge(xe_copied, b // 2 - 1)
                for t in range(NT):
                    last = pe.matmul(bank[:, (b % 2) * T:(b % 2 + 1) * T], xn_all[:, b * NT + t, :],
                                     disp[:, b * NT + t, :], start=(t == 0), stop=(t == NT - 1))
                if b % 2:
                    last.then_inc(xe_ready, 1)
                if b >= 2:
                    pe.wait_ge(dT_copied, b - 1)
                for g in range(2):
                    for t in range(NT):
                        last = pe.transpose(ps_m[b % 2][:, g * T + t * P:g * T + (t + 1) * P],
                                            disp[:, b * NT + t, g * P:(g + 1) * P], ident[:, :])
                last.then_inc(dT_ready, 1)

            def hidden(e):
                for f2 in range(2):
                    n = 2 * e + f2
                    if n >= NS:
                        pe.wait_ge(h_gelu, n - NS + 1)
                    for f in range(2):
                        col = slice((2 * f2 + f) * P, (2 * f2 + f + 1) * P)
                        last = pe.matmul(ps_s[n % NS][:, f * T:(f + 1) * T], w1_sb[:, e, col],
                                         xe[:, e, :, :].rearrange("p b s -> p (b s)"), start=True, stop=True)
                    last.then_inc(h_ready, 1)

            pe.wait_ge(xe_copied, B // 2)
            hidden(0)
            for e in range(E):
                if e + 1 < E:
                    hidden(e + 1)
                pe.wait_ge(h_gelu, 2 * e + 2)
                if e >= 2:
                    pe.wait_ge(y_copied, e - 1)
                for f in range(NF):
                    last = pe.matmul(ps_y[e % 2][:, 0:T], w2_sb[:, e, f, :], hid[e % 2][:, f * T:(f + 1) * T],
                                     start=(f == 0), stop=(f == NF - 1))
                last.then_inc(y_ready, 1)
            pe.wait_ge(y_copied, E)

            def turn(n):
                if n >= 2:
                    pe.wait_ge(ys_copied, n - 1)
                for b in range(2):
                    for g in range(2):
                        last = pe.transpose(ps_t[n % 2][:, (2 * b + g) * P:(2 * b + g + 1) * P],
                                            yT[:, 2 * n + b, 4 * g:4 * g + 4, :].rearrange("p e s -> p (e s)"), ident[:, :])
                last.then_inc(ys_ready, 1)

            pe.wait_ge(dT_copied, B)
            turn(0)
            for n in range(B // 2):
                if n + 1 < B // 2:
                    turn(n + 1)
                pe.wait_ge(ys_copied, n + 1)
                for b in (2 * n, 2 * n + 1):
                    if b >= 2:
                        pe.wait_ge(out_ready, b - 1)
                    for t in range(NT):
                        for g in range(2):
                            last = pe.matmul(ps_m[b % 2][:, t * P:(t + 1) * P], dT[:, b, g * T + t * P:g * T + (t + 1) * P],
                                             ys[:, b, g, :], start=(g == 0), stop=(g == 1))
                    last.then_inc(c_ready, 1)

        @block.vector
        def _(dve):
            def ln_stats(b, i):
                n = ln_number(b, i)
                rows = batch_rows(i if b else i + 1)
                dve.wait_ge(x_loaded, 16 if isinstance(i, int) and i == -1 else 32)
                if b:
                    wait_apart(dve, x1_step, i + 1)
                for t in range(NT):
                    dve.bn_stats(stats[:, b, t, :],
                                 x_all[:, bass.ds(rows + t, 1), :].rearrange("p a c -> p (a c)")).then_inc(ln_stat[b], 1)
                wait_apart(dve, ln_stat[b], n * NT + NT)
                for t in range(NT):
                    dve.bn_aggr(mv[:, b, t, :], stats[:, b, t, :]).then_inc(ln_mv[b], 1)

            def ln_apply(b, i):
                n = ln_number(b, i)
                rows = batch_rows(i if b else i + 1)
                dst = xn1 if b else xn0
                dve.wait_ge(ln_rstd[b], n + 1)
                if b and not (isinstance(i, int) and i == 0):
                    dve.wait_ge(xn_saved, i * 16)
                for t in range(NT):
                    ins = dve.tensor_scalar(dst[:, t, :], x_all[:, bass.ds(rows + t, 1), :].rearrange("p a c -> p (a c)"),
                                            mv[:, b, t, 0:1], rstd[:, b, t:t + 1], ALU.subtract, ALU.mult)
                ins.then_inc(xn_ready[b], 1)

            def task(kind, i, what, m, bank, place):
                if what in ("q0", "kT", "v1", "vT"):
                    return
                o = ps_m[bank]
                dve.wait_ge(m_ready[bank], task_base(i, bank) + place)
                if what == "xT0" or what == "xT1":
                    n = int(what == "xT1")
                    dve.wait_ge(xt_hi[n], ln_number(n, i) + 1)
                    dst = xT0 if what == "xT0" else xT1
                    ins = dve.tensor_tensor(dst[:, 1, :], o[:, 0:T], dst[:, 0, :].bitcast(F32), ALU.subtract)
                elif what == "k0":
                    ins = dve.tensor_copy(k_pair[:, 2 * m:2 * m + 2, :].rearrange("p j t -> p (j t)"), o[:, :])
                elif what == "v0":
                    t, f = m // 2, m % 2
                    ins = dve.tensor_copy(v_pair[:, t, 4 * f:4 * f + 4, 0:3:2, :],
                                          o[:, :].rearrange("p (j a d) -> p j a d", j=4, a=2))
                elif what == "q1":
                    ins = dve.tensor_tensor(q_rot[:, :, :, m, :].rearrange("p h a t -> p a h t"),
                                            o[:, :].rearrange("p (a h t) -> p a h t", a=2, h=H),
                                            rope_q[:, m, :, :].unsqueeze(2).broadcast_to([P, 2, H, TPH]), ALU.mult)
                elif what == "k1":
                    f, t = m // 2, m % 2
                    if m:
                        dve.wait_ge(k_rot, (i - 1) * 4 + m)
                    dve.tensor_tensor(k_cos.rearrange("p (a b) -> p a b", b=2),
                                      o[:, :].rearrange("p (a b) -> p a b", b=2),
                                      cos_k[:, f * 256:(f + 1) * 256].unsqueeze(2).broadcast_to([P, 256, 2]), ALU.mult)
                    s = sin_k[:, f * 256:(f + 1) * 256]
                    d = k_sin.rearrange("p (a b) -> p a b", b=2)
                    ov = o[:, :].rearrange("p (a b) -> p a b", b=2)
                    dve.scalar_tensor_tensor(d[:, :, 0], ov[:, :, 1], -1.0, s, ALU.mult, ALU.mult)
                    ins = dve.tensor_tensor(d[:, :, 1], ov[:, :, 0], s, ALU.mult)
                elif what == "proj0":
                    rows = x_all[:, bass.ds(batch_rows(i), NT), :]
                    ins = dve.tensor_tensor(rows, o[:, 0:NT * C].rearrange("p (t c) -> p t c", t=NT), rows, ALU.add)
                    ins.then_inc(m_done[bank], 1)
                    dve.wait_ge(m_done[bank], task_base(i, bank) + place)
                    ins = dve.tensor_tensor(rows, rows, bias[:, :].unsqueeze(1).broadcast_to([P, NT, C]), ALU.add)
                    ins.then_inc(x1_step, 1)
                    return
                elif what == "proj1":
                    rows = x_all[:, bass.ds(batch_rows(i - 1), NT), :]
                    ins = dve.tensor_tensor(rows, o[:, 0:NT * C].rearrange("p (t c) -> p t c", t=NT), rows, ALU.add)
                elif what == "logit":
                    ins = dve.tensor_copy(lg_all[:, bass.ds(batch_rows(i), NT), :],
                                          o[:, 0:NT * E].rearrange("p (t e) -> p t e", t=NT))
                ins.then_inc(m_done[bank], 1)

            def maxima(kind, i, k):
                o, nm = ps_s[k % NS], nmax[:, k % NS, :]
                dve.wait_ge(const_loaded, 16 * N_CONST)
                wait_apart(dve, s_ready, head_base(i) + k + 1)
                if k < heads_a(kind):
                    dve.tensor_tensor_reduce(o[:, 0:P], o[:, 0:P], mask[:, P:T], -1.0, BIG, ALU.add, ALU.min, nm[:, 0:1])
                    ins = dve.tensor_tensor_reduce(o[:, P:384], o[:, P:384], mask[:, :], -1.0, BIG, ALU.add,
                                                   ALU.min, nm[:, 1:2])
                else:
                    ins = dve.tensor_reduce(nm, o[:, :].rearrange("p (a t) -> p a t", a=2), AX.X, ALU.max, negate=True)
                ins.then_inc(max_ready, 1)

            def iteration(kind, i):
                for what, m, bank, place in schedule(kind):
                    if what == "S":
                        maxima(kind, i, m)
                    elif what == "R":
                        dve.wait_ge(p_ready, head_base(i) + m + 1)
                        dve.reciprocal(rinv[:, m % NS, :], rsum[:, m % NS, :]).then_inc(rinv_ready, 1)
                    elif what == "T" and m % 2 == 1:
                        dve.wait_ge(t_ready, head_base(i) + m + 1)
                        if m >= NPT:
                            dve.wait_ge(pv_done, head_base(i) + m - NPT + 1)
                        n = 384 if m < heads_a(kind) else 512
                        dve.tensor_copy(probT[:, m % NPT, 0:n], ps_t[m % NPT][:, 0:n]).then_inc(t_copied[1], 1)
                    elif what == "stat":
                        ln_stats(m, i)
                    elif what == "norm":
                        ln_apply(m, i)
                    elif bank is not None:
                        task(kind, i, what, m, bank, place)

            dve.memset(v_pair[:, :, :, 1, :], 0.0).then_inc(zeroed, 1)
            dve.memset(half_pow[:, :], -0.5).then_inc(zeroed, 1)
            dve.memset(ones[:, :], 1.0).then_inc(zeroed, 1)
            dve.wait_ge(wf_loaded, 48)
            wf = prob[:, 0, 0:C]
            dve.tensor_reduce(thr[:, 0:1], wf, AX.X, ALU.add, apply_absolute_value=True).then_inc(thr_step, 1)
            dve.wait_ge(w0_hi, 1)
            dve.tensor_tensor(w0[:, 1, :, :].rearrange("p a n -> p (a n)"), q_flat[:, 0:3 * HD],
                              w0[:, 0, :, :].rearrange("p a n -> p (a n)").bitcast(F32), ALU.subtract).then_inc(w0_split, 1)
            iteration(PRO, -1)
            dve.wait_ge(abs_sum, 1)
            dve.tensor_scalar(thr[:, 1:2], ps_t[0][:, 0:1], THRESH / (C * C), None, ALU.mult).then_inc(thr_step, 1)
            dve.wait_ge(thr_step, 2)
            dve.tensor_scalar(thr[:, 2:3], thr[:, 1:2], -1.0, None, ALU.mult).then_inc(thr_step, 1)
            dve.tensor_scalar(prob[:, 1, 0:C], wf, thr[:, 1:2], None, ALU.is_gt).then_inc(thr_step, 1)
            dve.wait_ge(thr_step, 4)
            dve.scalar_tensor_tensor(prob[:, 1, C:2 * C], wf, thr[:, 2:3], prob[:, 1, 0:C], ALU.is_lt, ALU.subtract).then_inc(thr_step, 1)
            dve.wait_ge(thr_step, 5)
            dve.tensor_scalar(prob[:, 2, 0:C], prob[:, 1, C:2 * C], alpha[:, 0:1], -1.0, ALU.mult, ALU.mult).then_inc(thr_step, 1)
            dve.wait_ge(thr_step, 6)
            dve.tensor_copy(we[:, 0, :], prob[:, 2, 0:C]).then_inc(thr_step, 1)
            dve.tensor_copy(wg[:, 0, :], prob[:, 0, C:C + E]).then_inc(thr_step, 1)
            dve.wait_ge(thr_step, 8)
            dve.tensor_tensor(we[:, 1, :], prob[:, 2, 0:C], we[:, 0, :].bitcast(F32), ALU.subtract).then_inc(wf_split, 1)
            dve.tensor_tensor(wg[:, 1, :], prob[:, 0, C:C + E], wg[:, 0, :].bitcast(F32), ALU.subtract).then_inc(wf_split, 1)
            iteration(FIRST, 0)
            dve.wait_ge(w1_hi, 2)
            dve.tensor_tensor(wq1[:, 1, :], k_flat[:, 0:2 * HD], wq1[:, 0, :].bitcast(F32), ALU.subtract)
            dve.tensor_tensor(wkv1[:, 1, :, :].rearrange("p a n -> p (a n)"), k_flat[:, 2 * HD:4 * HD],
                              wkv1[:, 0, :, :].rearrange("p a n -> p (a n)").bitcast(F32), ALU.subtract).then_inc(w1_split, 1)
            with dve.Fori(I_LOOP, I_NO_NEXT) as i:
                iteration(FULL, i)
            iteration(NO_NEXT, I_NO_NEXT)
            iteration(LAST, I_LAST)

            steps = [0]

            def then(ins):
                steps[0] += 1
                ins.then_inc(route, 1)
                dve.wait_ge(route, steps[0])

            def wider(a):
                return a.unsqueeze(2).broadcast_to([P, B * NT, E])

            top, total, inv, gate, best, pos, off, keep, slot = thin[0:9]
            logits = lg_all[:, :, :]
            dve.wait_ge(experts_loaded, 16 * (E + 2))
            then(dve.tensor_reduce(top, logits, AX.X, ALU.max))
            then(dve.tensor_tensor(wide[0], logits, wider(top), ALU.subtract))
            dve.wait_ge(route_exp, 1)
            then(dve.tensor_reduce(total, wide[1], AX.X, ALU.add))
            then(dve.reciprocal(inv, total))
            then(dve.tensor_tensor(wide[2], wide[1], wider(inv), ALU.mult))
            then(dve.tensor_reduce(gate, wide[2], AX.X, ALU.max))
            then(dve.tensor_tensor(wide[3], wide[2], wider(gate), ALU.is_equal))
            then(dve.tensor_tensor(wide[4], wide[3], rank, ALU.mult))
            then(dve.tensor_reduce(best, wide[4], AX.X, ALU.max))
            then(dve.tensor_tensor(wide[5], wide[4], wider(best), ALU.is_equal))
            assert steps[0] == ROUTE_MASK
            then(dve.tensor_tensor(wide[7], wide[5], first_slot, ALU.mult))
            then(dve.tensor_reduce(off, wide[7], AX.X, ALU.add))
            dve.wait_ge(pos_ready, 1)
            then(dve.tensor_tensor(wide[6].rearrange("p (b t) e -> p t b e", t=NT),
                                   ps_s[0][:, 0:2 * B * E].rearrange("p (t b e) -> p t b e", t=NT, b=B),
                                   wide[5].rearrange("p (b t) e -> p t b e", t=NT), ALU.mult))
            then(dve.tensor_reduce(pos, wide[6], AX.X, ALU.add))
            then(dve.tensor_scalar(keep, pos, float(CAP), None, ALU.is_lt))
            then(dve.tensor_tensor(slot, pos, off, ALU.add))
            then(dve.scalar_tensor_tensor(slot, slot, 1.0, keep, ALU.add, ALU.mult))
            then(dve.tensor_scalar(slot, slot, -1.0, None, ALU.add))
            for n in range(B * NT):
                dve.tensor_scalar(disp[:, n, :], iota, slot[:, n:n + 1], None, ALU.is_equal).then_inc(disp_ready, 1)
            for b in range(B):
                dve.wait_ge(dT_ready, b + 1)
                dve.tensor_copy(dT[:, b, :], ps_m[b % 2][:, :]).then_inc(dT_copied, 1)
            for e in range(E):
                dve.wait_ge(y_ready, e + 1)
                dve.tensor_copy(yT[:, :, e, :], ps_y[e % 2][:, 0:T].rearrange("p (b s) -> p b s", b=B)).then_inc(y_copied, 1)
            for b in range(B):
                dve.wait_ge(c_ready, b + 1)
                for t in range(NT):
                    n = b * NT + t
                    ins = dve.scalar_tensor_tensor(x_all[:, n, :], ps_m[b % 2][:, t * P:(t + 1) * P], gate[:, n:n + 1],
                                                   x_all[:, n, :], ALU.mult, ALU.add)
                ins.then_inc(out_ready, 1)

        @block.scalar
        def _(act):
            def task(kind, i, what, m, bank, place):
                o = ps_m[bank]
                if what not in ("xT0", "xT1", "q0", "kT", "v1", "vT"):
                    return
                act.wait_ge(m_ready[bank], task_base(i, bank) + place)
                if what == "xT0" or what == "xT1":
                    dst = xT0 if what == "xT0" else xT1
                    act.activation(dst[:, 0, :], o[:, 0:T], ACT.Copy).then_inc(xt_hi[int(what == "xT1")], 1)
                    return
                if what == "q0":
                    for hh in range(2):
                        rows = slice(hh * DK, (hh + 1) * DK)
                        ins = act.activation(q_pad[rows, 2 * m:2 * m + 2, hh, :],
                                             o[rows, :].rearrange("p (j t) -> p j t", j=2), ACT.Copy, scale=float(DK) ** 0.5)
                elif what == "kT":
                    ins = act.activation(k_dup[:, :, :, m, :].rearrange("p h a t -> p a h t"),
                                         o[:, :].rearrange("p (a h t) -> p a h t", a=2, h=H), ACT.Copy)
                elif what == "v1":
                    ins = act.activation(v_col[:, :, 2 * m * TPH:(2 * m + 2) * TPH].rearrange("p h (j t) -> p j h t", j=2),
                                         o[:, :].rearrange("p (j h t) -> p j h t", j=2, h=H), ACT.Copy)
                elif what == "vT":
                    ins = act.activation(v_row[:, 64 + 8 * P * m:64 + 8 * P * (m + 1)].rearrange("p (a d) -> p a d", d=P)[:, :, 0:DK],
                                         o[:, :].rearrange("p (a d) -> p a d", d=DK), ACT.Copy)
                ins.then_inc(m_done[bank], 1)

            def exps(kind, i, k):
                o, nm, rs = ps_s[k % NS], nmax[:, k % NS, :], rsum[:, k % NS, :]
                p = prob[:, k % NP_, :]
                act.wait_ge(max_ready, head_base(i) + k + 1)
                if k >= NP_:
                    act.wait_ge(t_ready, head_base(i) + k - NP_ + 1)
                if k < heads_a(kind):
                    parts, scale = [(0, P), (P, 384)], -1.0
                else:
                    parts, scale = [(0, T), (T, 2 * T)], 1.0
                for n, (lo, hi) in enumerate(parts):
                    ins = act.activation(p[:, lo:hi], o[:, lo:hi], ACT.Exp, bias=nm[:, n:n + 1], scale=scale,
                                         accum_out=rs[:, n:n + 1])
                ins.then_inc(p_ready, 1)

            def iteration(kind, i):
                for what, m, bank, place in schedule(kind):
                    if what == "S":
                        exps(kind, i, m)
                    elif what == "T" and m % 2 == 0:
                        act.wait_ge(t_ready, head_base(i) + m + 1)
                        if m >= NPT:
                            act.wait_ge(pv_done, head_base(i) + m - NPT + 1)
                        n = 384 if m < heads_a(kind) else 512
                        act.activation(probT[:, m % NPT, 0:n], ps_t[m % NPT][:, 0:n], ACT.Copy).then_inc(t_copied[0], 1)
                    elif what == "O":
                        act.wait_ge(pv_done, head_base(i) + 2 * m + 2)
                        src, p2 = ps_o[:, 0:T], m % NJ
                        if 2 * m < heads_a(kind):
                            ins = act.activation(oT[:, p2, :], src, ACT.Copy)
                        else:
                            ins = act.activation(oT[:, :, 2 * p2 * TPH:(2 * p2 + 2) * TPH].rearrange("p j (h t) -> p h j t", h=2),
                                                 src.rearrange("p (h j t) -> p h j t", h=2, j=NJ), ACT.Copy)
                        ins.then_inc(o_copied, 1)
                    elif bank is not None:
                        task(kind, i, what, m, bank, place)

            act.wait_ge(w0_loaded, 16)
            act.activation(w0[:, 0, :, :].rearrange("p a n -> p (a n)"), q_flat[:, 0:3 * HD], ACT.Copy).then_inc(w0_hi, 1)
            iteration(PRO, -1)
            act.wait_ge(w1_loaded, 16)
            act.activation(wq1[:, 0, :], k_flat[:, 0:2 * HD], ACT.Copy).then_inc(w1_hi, 1)
            act.activation(wkv1[:, 0, :, :].rearrange("p a n -> p (a n)"), k_flat[:, 2 * HD:4 * HD], ACT.Copy).then_inc(w1_hi, 1)
            act.wait_ge(wf_split, 2)
            iteration(FIRST, 0)
            with act.Fori(I_LOOP, I_NO_NEXT) as i:
                iteration(FULL, i)
            iteration(NO_NEXT, I_NO_NEXT)
            iteration(LAST, I_LAST)

            act.wait_ge(route, 2)
            act.activation(wide[1], wide[0], ACT.Exp).then_inc(route_exp, 1)
            for n in range(B // 2):
                act.wait_ge(xe_ready, n + 1)
                act.activation(xe[:, :, 2 * n:2 * n + 2, :].rearrange("p e b s -> p b e s"),
                               ps_t[n % 2][:, :].rearrange("p (b e s) -> p b e s", b=2, e=E), ACT.Copy).then_inc(xe_copied, 1)
            for n in range(2 * E):
                act.wait_ge(h_ready, n + 1)
                e, f2 = n // 2, n % 2
                if e >= 2:
                    act.wait_ge(y_ready, e - 1)
                act.activation(hid[e % 2][:, f2 * 512:(f2 + 1) * 512], ps_s[n % NS][:, :], ACT.Gelu_apprx_tanh).then_inc(h_gelu, 1)
            for n in range(B // 2):
                act.wait_ge(ys_ready, n + 1)
                act.activation(ys[:, 2 * n:2 * n + 2, :, :].rearrange("p b g d -> p (b g d)"), ps_t[n % 2][:, :],
                               ACT.Copy).then_inc(ys_copied, 1)

        @block.gpsimd
        def _(pool):
            def iteration(kind, i):
                for what, m, bank, place in schedule(kind):
                    if what == "R":
                        p, r = prob[:, m % NP_, :], rinv[:, m % NS, :]
                        pool.wait_ge(rinv_ready, head_base(i) + m + 1)
                        if m < heads_a(kind):
                            pool.tensor_tensor(p[:, 0:P], p[:, 0:P], r[:, 0:1].broadcast_to([P, P]), ALU.mult)
                            ins = pool.tensor_tensor(p[:, P:384], p[:, P:384], r[:, 1:2].broadcast_to([P, T]), ALU.mult)
                        else:
                            pv = p.rearrange("p (a t) -> p a t", a=2)
                            ins = pool.tensor_tensor(pv, pv, r.unsqueeze(2).broadcast_to([P, 2, T]), ALU.mult)
                        ins.then_inc(norm_ready, 1)
                    elif what == "stat":
                        n = ln_number(m, i)
                        wait_apart(pool, ln_mv[m], n * NT + NT)
                        pool.tensor_scalar(vareps[:, m, :], mv[:, m, :, 1], EPS, None, ALU.add).then_inc(ln_eps[m], 1)
                        pool.wait_ge(ln_eps[m], n + 1)
                        pool.tensor_tensor(rstd[:, m, :], vareps[:, m, :], half_pow[:, :], ALU.pow).then_inc(ln_rstd[m], 1)
                    elif what == "k1":
                        t = m % 2
                        pool.wait_ge(m_done[bank], task_base(i, bank) + place)
                        both = [x.rearrange("p (c d) -> p c d", d=DK).unsqueeze(2).broadcast_to([P, H // 2, 2, DK])
                                for x in (k_cos, k_sin)]
                        pool.tensor_tensor(k_tok[:, t, :, :, :], *both, ALU.add).then_inc(k_rot, 1)

            pool.memset(q_pad[:, :, :, :], 0.0).then_inc(zeroed, 1)
            pool.memset(v_row[:, :], 0.0).then_inc(zeroed, 1)
            pool.wait_ge(zeroed, 5)
            iteration(PRO, -1)
            iteration(FIRST, 0)
            with pool.Fori(I_LOOP, I_NO_NEXT) as i:
                iteration(FULL, i)
            iteration(NO_NEXT, I_NO_NEXT)
            iteration(LAST, I_LAST)


_INS = ["x", "w0", "w1", "wf", "wg", "alpha", "bias", "lin", "wo", "We1", "We2",
        "ident", "mask", "rope_q", "cos_k", "sin_k", "routing"]


def constants():
    inv = 1.0 / 10000.0 ** (np.arange(0, DK, 2, dtype=np.float32) / DK)
    ang = np.outer(np.arange(T, dtype=np.float32), inv.astype(np.float32))
    cos = np.ones((T, DK // 2), np.float32)
    sin = np.zeros((T, DK // 2), np.float32)
    cos[1:], sin[1:] = np.cos(ang[:T - 1]), np.sin(ang[:T - 1])
    pos = np.arange(T).reshape(TPH, H)
    signed = np.stack([-sin, sin], -1).reshape(T, DK)
    both = np.concatenate([np.repeat(cos, 2, 1), signed], 1) / np.float32(DK ** 0.5)
    rope_q = both[pos.T.reshape(NJ, 2, TPH)].transpose(3, 0, 1, 2).reshape(P, T)
    rows = pos[np.arange(P) % TPH]
    cos_k, sin_k = cos[rows].reshape(P, HD // 2), sin[rows].reshape(P, HD // 2)
    q, k = np.arange(P)[:, None], np.arange(T)[None, :]
    mask = np.where(k > q + P, NEG, 0)
    upper = (np.arange(P)[:, None] < np.arange(P)[None, :])
    iota = np.tile(np.arange(E * CAP), (P, 1))
    first = np.tile(np.arange(E) * CAP, (P, B * NT))
    rank = np.tile(E - np.arange(E), (P, B * NT))
    routing = np.concatenate([upper, iota, first, rank], 1)
    return {n: np.ascontiguousarray(a, np.float32) for n, a in dict(
        ident=np.eye(P), mask=mask, rope_q=rope_q, cos_k=cos_k, sin_k=sin_k, routing=routing).items()}


def laid_out(a):
    rows = lambda w: np.asarray(w).reshape(C, HD)
    cols = lambda w: np.asarray(w).T
    q1 = cols(a["L1_attn_wq"]).reshape(C, H, 1, DK // 2, 2)
    q1 = np.concatenate([q1, q1[..., ::-1]], 2).reshape(C, 2 * HD)
    d = dict(
        x=a["L0_attn_x"],
        w0=np.concatenate([rows(a["L0_attn_query_mat"]), rows(a["L0_attn_key_mat"]), rows(a["L0_attn_value_mat"])], 1),
        w1=np.concatenate([q1, cols(a["L1_attn_wk"]), cols(a["L1_attn_wv"])], 1),
        wf=cols(a["L0_ffn_weight"]), wg=a["L1_ffn_Wg"],
        alpha=np.broadcast_to(np.asarray(a["L0_ffn_alpha"]), (P, 1)),
        bias=np.broadcast_to(np.asarray(a["L0_ffn_bias"]), (P, C)),
        lin=a["L0_attn_linear_m1"], wo=cols(a["L1_attn_wo"]), We1=a["L1_ffn_W1"], We2=a["L1_ffn_W2"])
    d.update(constants())
    return {n: np.ascontiguousarray(d[n]) for n in _INS}


def kernel(**inputs):
    import concourse.bacc as bacc
    from concourse.bass_utils import run_bass_kernel_spmd as run

    nc = bacc.Bacc("TRN2", target_bir_lowering=False, num_devices=1)
    arrays, aps = {}, {}
    for name, a in laid_out(inputs).items():
        arrays[f"in_{name}_dram"] = a
        aps[name] = nc.dram_tensor(f"in_{name}_dram", a.shape, mybir.dt.from_np(a.dtype), kind="ExternalInput").ap()
    out = nc.dram_tensor("out_0_dram", (B, T, C), F32, kind="ExternalOutput").ap()
    build(nc, aps, out)
    r = run(nc, [arrays], core_ids=[0])
    return r.results[0]["out_0_dram"]
```

```python
from contextlib import ExitStack

import numpy as np

import concourse.bass as bass
from concourse import mybir

P = 128
B, T, C = 8, 256, 128
H, DK = 16, 64
HD = H * DK
NT = T // P
NJ = H // 2
TPH = T // H
E, FF, CAP = 8, 512, T // 8
NF = FF // P
EPS = 1e-5
N_CONST = 6
THRESH = 0.7
NEG = -1.0e30
BIG = 3.0e38

F32 = mybir.dt.float32
F32R = mybir.dt.float32r
ALU = mybir.AluOpType
ACT = mybir.ActivationFunctionType
AX = mybir.AxisListType

NS, NP_, NPT = 3, 3, 2

ROUTE_MASK = 10

PRO, FIRST, FULL, NO_NEXT, LAST = range(5)
I_LOOP, I_NO_NEXT, I_LAST = 1, B - 1, B

QKV1 = [(0, "v1", 0), (1.5, "v1", 1), (2, "v1", 2), (2.5, "v1", 3), (3, "vT", 1), (3.5, "vT", 2), (4, "vT", 3),
        (5, "vT", 0), (5, "k1", 0), (6, "k1", 1), (6, "q1", 3), (8, "q1", 2), (8, "kT", 0), (9, "q1", 7),
        (9.5, "kT", 1), (10, "q1", 5), (10.5, "q1", 1), (11, "k1", 2), (12, "k1", 3), (13, "q1", 6), (14, "q1", 0),
        (14, "q1", 4), (14, "kT", 2), (14, "kT", 3)]
A_TASKS = [(4, "stat", 0), (20, "proj0", 0), (20.5, "norm", 0), (21, "stat", 1), (21.5, "xT0", 0), (29.5, "norm", 1),
           (33.5, "xT1", 0), (38, "logit", 0)]
QKV0 = [(22.5, "v0", 2), (24, "k0", 2), (26, "v0", 1), (27, "q0", 0), (27.5, "k0", 0), (29, "k0", 3), (31, "q0", 3),
        (32, "k0", 1), (32.5, "v0", 3), (33, "q0", 2), (33.5, "v0", 0), (34.5, "q0", 1)]
PRO_TASKS = [("stat", 0), ("zeros", 0), ("norm", 0), ("w0", 0), ("xT0", 0), ("w0", 1), ("w0", 2), ("q0", 0), ("k0", 0), ("v0", 0),
             ("q0", 1), ("k0", 1), ("v0", 1), ("q0", 2), ("k0", 2), ("v0", 2), ("q0", 3), ("k0", 3), ("v0", 3)]
FIRST_TASKS = [(1.5, "wf", 0), (H - 4, "stat", 0), (H - 3, "norm", 0)] + [
    (3.5 + n, "w1hi", n) for n in range(8)] + [(4.5 + n, "w1lo", n) for n in range(8)] + [
    (H + 4, *t) for t in [("proj0", 0), ("xT0", 0), ("q0", 0), ("k0", 0), ("stat", 1), ("v0", 0), ("q0", 1), ("k0", 1),
                          ("norm", 1), ("v0", 1), ("q0", 2), ("k0", 2), ("xT1", 0), ("v0", 2), ("q0", 3), ("k0", 3),
                          ("v0", 3), ("logit", 0)]]


def schedule(kind):
    a = H if kind in (FIRST, FULL, NO_NEXT) else 0
    b = H if kind in (FULL, NO_NEXT, LAST) else 0
    n = a + b
    tasks = []
    if kind == PRO:
        tasks += [(0, *t) for t in PRO_TASKS]
    if kind == LAST:
        tasks += [(-1, *t[1:]) for t in QKV1]
    if kind in (FULL, NO_NEXT):
        tasks += QKV1
    if kind == FIRST:
        tasks += FIRST_TASKS
    elif a:
        tasks += [t for t in A_TASKS if kind != NO_NEXT or t[1:] not in (("stat", 0), ("norm", 0), ("xT0", 0))]
    if kind == FULL:
        tasks += QKV0
    if b:
        tasks.append((n + 3.5, "proj1", 0))
    out = []
    for s in range(int(min(0, tasks[0][0])), int(max([t[0] for t in tasks] + [n + 3 if n else 0])) + 1):
        if 0 <= s < n:
            out.append(("S", s))
        if 0 <= s - 1 < n:
            out.append(("R", s - 1))
        out += [t[1:] for t in tasks if t[0] == s]
        if 0 <= s - 2 < n:
            out.append(("T", s - 2))
        if 0 <= s - 3 < n:
            out.append(("PV", s - 3))
            if (s - 3) % 2:
                out.append(("O", (s - 3) // 2))
        out += [t[1:] for t in tasks if t[0] == s + 0.5]
    assert all(t[1:] in out for t in tasks)
    done, placed = [0, 0], []
    for what, m in out:
        if what in TASKS:
            bank = sum(done) % 2
            done[bank] += 1
            placed.append((what, m, bank, done[bank]))
        else:
            placed.append((what, m, None, None))
    return placed


TASKS = ("xT0", "q0", "k0", "v0", "proj0", "xT1", "logit", "q1", "k1", "kT", "v1", "vT", "proj1")


def tasks_in(kind, bank):
    return sum(1 for x in schedule(kind) if x[2] == bank)


def task_base(i, bank):
    if isinstance(i, int) and i < 1:
        return 0 if i == -1 else tasks_in(PRO, bank)
    before = tasks_in(PRO, bank) + tasks_in(FIRST, bank)
    if isinstance(i, int) and i == I_LAST:
        return before + (I_NO_NEXT - 1) * tasks_in(FULL, bank) + tasks_in(NO_NEXT, bank)
    return (i - 1) * tasks_in(FULL, bank) + before


def head_base(i):
    return 0 if isinstance(i, int) and i < 1 else i * (2 * H) - H


def pair_base(i):
    return 0 if isinstance(i, int) and i < 1 else i * H - NJ


def batch_rows(i):
    return i * NT


def heads_a(kind):
    return 0 if kind in (PRO, LAST) else H


def task_at(kind, name, m):
    for what, n, bank, place in schedule(kind):
        if (what, n) == (name, m):
            return bank, place
    raise ValueError((kind, name, m))


def order(name, kind):
    return [x[1] for x in schedule(kind) if x[0] == name]


def is_first(kind, names, what, m):
    return what in names and (what, m) == [x[:2] for x in schedule(kind) if x[0] in names][0]


def build(nc, t_in, out):
    ctx = ExitStack()
    with ctx:
        def sb(name, shape, dt=F32):
            return ctx.enter_context(nc.sbuf_tensor(name, shape, dt))

        def sem(name):
            return ctx.enter_context(nc.semaphore(name))

        w0 = sb("w0", [P, 2, 3, HD], F32R)
        wq1 = sb("wq1", [P, 2, 2 * HD], F32R)
        wkv1 = sb("wkv1", [P, 2, 2, HD], F32R)
        we = sb("we", [P, 2, C], F32R)
        wg = sb("wg", [P, 2, E], F32R)
        lin = sb("lin", [P, NJ, C])
        wo = sb("wo", [P, NJ, C])
        mem0 = sb("mem0", [P, 4096 + 2048 + 3072])
        q_pad = mem0[:, 0:4096].rearrange("p (j a t) -> p j a t", j=NJ, a=2)
        k_pair = mem0[:, 4096:6144].rearrange("p (j t) -> p j t", j=NJ)
        v_pair = mem0[:, 6144:9216].rearrange("p (b j a d) -> p b j a d", b=NT, j=NJ, a=3)
        w1_sb = mem0[:, 0:4096].rearrange("p (e f) -> p e f", e=E)
        w2_sb = mem0[:, 4096:8192].rearrange("p (e f d) -> p e f d", e=E, f=NF)
        q_rot = sb("q_rot", [P, H, 2, NJ, TPH])
        k_dup = sb("k_dup", [P, H, 2, NJ, TPH])
        q_flat = q_rot[:, :, :, :, :].rearrange("p h a j t -> p (h a j t)")
        k_flat = k_dup[:, :, :, :, :].rearrange("p h a j t -> p (h a j t)")
        v_row = sb("v_row", [P, 64 + 2 * H * P])
        v_col = sb("v_col", [P, H, P])
        k_tok = sb("k_tok", [P, NT, HD // 2])
        wf_raw, we_sign, we_full, wf_above = [k_tok[:, 0, n * C:(n + 1) * C] for n in range(4)]
        wg_raw = k_tok[:, 1, 0:E]
        k_cos = v_col[:, 0:4, :].rearrange("p a b -> p (a b)")
        k_sin = v_col[:, 4:8, :].rearrange("p a b -> p (a b)")
        x_all = sb("x_all", [P, B * NT, C])
        lg_all = sb("lg_all", [P, B * NT, E])
        xn0 = sb("xn0", [P, NT, C])
        xn1 = sb("xn1", [P, NT, C])
        xT0 = sb("xT0", [P, 2, T], F32R)
        xT1 = sb("xT1", [P, 2, T], F32R)
        prob = sb("prob", [P, NP_, 512])
        probT = sb("probT", [P, NPT, 512])
        oT = sb("oT", [P, NJ, T])
        nmax = sb("nmax", [P, NS, 2])
        rsum = sb("rsum", [P, NS, 2])
        rinv = sb("rinv", [P, NS, 2])
        stats = sb("stats", [P, 2, NT, 6])
        mv = sb("mv", [P, 2, NT, 2])
        vareps = sb("vareps", [P, 2, NT])
        rstd = sb("rstd", [P, 2, NT])
        ident = sb("ident", [P, P])
        mask = sb("mask", [P, T])
        rope_q = sb("rope_q", [P, NJ, 2, TPH])
        cos_k = sb("cos_k", [P, HD // 2])
        sin_k = sb("sin_k", [P, HD // 2])
        bias = sb("bias", [P, C])
        alpha = sb("alpha", [P, 1])
        ones = sb("ones", [P, P])
        half_pow = sb("half_pow", [P, NT])
        thr = sb("thr", [P, 4])

        ps_s = [ctx.enter_context(nc.psum_tensor(f"ps_s{n}", [P, 512], F32)) for n in range(NS)]
        ps_t = [ctx.enter_context(nc.psum_tensor(f"ps_t{n}", [P, 512], F32)) for n in range(NPT)]
        ps_o = ctx.enter_context(nc.psum_tensor("ps_o", [P, 512], F32))
        ps_m = [ctx.enter_context(nc.psum_tensor(f"ps_m{n}", [P, 512], F32)) for n in range(2)]

        xn_dram = nc.dram_tensor("xn_dram", (B, P, NT * C), F32)

        x_loaded = [sem(f"x_loaded{n}") for n in range(2)]
        ident_loaded = sem("ident_loaded")
        w0_loaded = [sem(f"w0_loaded{n}") for n in range(3)]
        w1_loaded = sem("w1_loaded")
        wf_loaded = [sem(f"wf_loaded{n}") for n in range(2)]
        const_loaded = sem("const_loaded")
        mask_loaded = sem("mask_loaded")
        experts_loaded = sem("experts_loaded")
        zeroed = sem("zeroed")
        pool_zeroed = sem("pool_zeroed")
        w0_hi, w0_split = sem("w0_hi"), sem("w0_split")
        w1_hi, w1_split = sem("w1_hi"), sem("w1_split")
        thr_step, abs_sum, wf_split = sem("thr_step"), sem("abs_sum"), sem("wf_split")
        s_ready = sem("s_ready")
        max_ready = sem("max_ready")
        p_ready = sem("p_ready")
        rinv_ready = sem("rinv_ready")
        norm_ready = sem("norm_ready")
        t_ready = sem("t_ready")
        t_copied = [sem(f"t_copied{n}") for n in range(2)]
        pv_done = sem("pv_done")
        o_copied = sem("o_copied")
        m_ready = [sem(f"m_ready{n}") for n in range(2)]
        m_done = [sem(f"m_done{n}") for n in range(2)]
        xt_hi = [sem(f"xt_hi{n}") for n in range(2)]
        even_copied = sem("even_copied")
        k_rot = sem("k_rot")
        x1_step = sem("x1_step")
        ln_stat, ln_mv, ln_eps, ln_rstd, xn_ready = [[sem(f"{what}{n}") for n in range(2)] for what in (
            "ln_stat", "ln_mv", "ln_eps", "ln_rstd", "xn_ready")]
        xn_saved = sem("xn_saved")
        passed = sem("passed")
        xn_loaded = sem("xn_loaded")
        route = sem("route")
        route_exp = sem("route_exp")
        pos_ready = sem("pos_ready")
        disp_ready = sem("disp_ready")
        xe_ready, xe_copied = sem("xe_ready"), sem("xe_copied")
        dT_ready, dT_copied = sem("dT_ready"), sem("dT_copied")
        h_ready, h_gelu = sem("h_ready"), sem("h_gelu")
        y_ready, y_copied = sem("y_ready"), sem("y_copied")
        ys_ready, ys_copied = sem("ys_ready"), sem("ys_copied")
        c_ready, out_ready = sem("c_ready"), sem("out_ready")
        out_stored = sem("out_stored")

        xn_all = v_col
        disp = q_flat.rearrange("p (n s) -> p n s", n=B * NT)
        xe = k_flat[:, 0:E * B * CAP].rearrange("p (e b s) -> p e b s", e=E, b=B)
        yT = k_flat[:, E * B * CAP:2 * E * B * CAP].rearrange("p (b e s) -> p b e s", b=B, e=E)
        dT = v_row[:, 0:B * 2 * T].rearrange("p (b f) -> p b f", b=B)
        ys = oT[:, :, :].rearrange("p j t -> p (j t)").rearrange("p (b g d) -> p b g d", b=B, g=2)
        ps_y = [ps_o, ps_t[0]]
        hid = [prob[:, 0:2, :].rearrange("p a f -> p (a f)"), probT[:, :, :].rearrange("p a f -> p (a f)")]
        upper = mem0[:, 8192:8320]
        iota = mem0[:, 8320:8576]
        first_slot = mem0[:, 8576:8704].rearrange("p (n e) -> p n e", e=E)
        rank = mem0[:, 8704:8832].rearrange("p (n e) -> p n e", e=E)
        wide = [x[:, n * 128:(n + 1) * 128].rearrange("p (n e) -> p n e", e=E) for x in (sin_k, cos_k) for n in range(4)]
        thin = [mask[:, n * 16:(n + 1) * 16] for n in range(10)]

        block = ctx.enter_context(nc.Block())

        def w1_part(n, low):
            half = slice(n % 2 * 512, (n % 2 + 1) * 512)
            return wq1[:, low, n * 512:(n + 1) * 512] if n < 4 else wkv1[:, low, n // 2 - 2, half]

        def turned_k(eng, kind, i, o, m, e):
            src = o[e * DK:(e + 1) * DK, :].rearrange("p (j h t) -> p j h t", j=2, h=H)
            for half in range(2):
                dst = k_dup[half * DK:(half + 1) * DK, :, e, 2 * m:2 * m + 2, :].rearrange("p h j t -> p j h t")
                if e == 0:
                    ins = eng.activation(dst, src, ACT.Copy)
                else:
                    if half:
                        eng.wait_ge(even_copied, (i - 1) * 4 + order("kT", kind).index(m) + 1)
                    ins = eng.tensor_copy(dst, src)
            if e == 0:
                ins.then_inc(even_copied, 1)
            return ins

        def wait_apart(eng, s, value):
            eng.wait_ge(s, value)
            if not isinstance(value, int):
                eng.sem_inc(passed, 1)

        def ln_number(block_no, i):
            return i if block_no else i + 1

        @block.sync
        def _(sp):
            xv = t_in["x"].rearrange("b (t p) c -> p (b t) c", p=P)
            sp.dma_start(x_all[:, 0:NT, :], xv[:, 0:NT, :]).then_inc(x_loaded[0], 16)
            sp.dma_start(wf_raw[:, :], t_in["wf"]).then_inc(wf_loaded[0], 16)
            sp.dma_start(q_flat[:, 0:HD], t_in["w0"][:, 0:HD]).then_inc(w0_loaded[0], 16)
            sp.dma_start(ident[:, :], t_in["ident"]).then_inc(ident_loaded, 16)
            for n in (1, 2):
                sp.dma_start(q_flat[:, n * HD:(n + 1) * HD], t_in["w0"][:, n * HD:(n + 1) * HD]).then_inc(w0_loaded[n], 16)
            sp.dma_start(wg_raw[:, :], t_in["wg"]).then_inc(wf_loaded[1], 16)
            sp.dma_start(alpha[:, :], t_in["alpha"]).then_inc(wf_loaded[1], 16)
            sp.dma_start(mask[:, :], t_in["mask"]).then_inc(mask_loaded, 16)
            sp.dma_start(x_all[:, NT:, :], xv[:, NT:, :]).then_inc(x_loaded[1], 16)
            sp.dma_start(bias[:, :], t_in["bias"]).then_inc(const_loaded, 16)
            sp.dma_start(lin[:, :, :], t_in["lin"].rearrange("(j p) z -> p j z", p=P)).then_inc(const_loaded, 16)
            sp.dma_start(k_flat, t_in["w1"]).then_inc(w1_loaded, 16)
            sp.dma_start(wo[:, :, :], t_in["wo"].rearrange("(j p) z -> p j z", p=P)).then_inc(const_loaded, 16)
            sp.dma_start(rope_q[:, :, :, :].rearrange("p j a t -> p (j a t)"), t_in["rope_q"]).then_inc(const_loaded, 16)
            sp.dma_start(cos_k[:, :], t_in["cos_k"]).then_inc(const_loaded, 16)
            sp.dma_start(sin_k[:, :], t_in["sin_k"]).then_inc(const_loaded, 16)
            with sp.Fori(0, B) as i:
                sp.wait_ge(xn_ready[1], i + 1)
                sp.dma_start(xn_dram[bass.ds(i, 1), :, :].rearrange("b p f -> p (b f)"),
                             xn1[:, :, :].rearrange("p t c -> p (t c)")).then_inc(xn_saved, 16)
            sp.wait_ge(xn_saved, 16 * B)

            sp.wait_ge(pv_done, head_base(I_NO_NEXT) + H)
            sp.wait_ge(s_ready, head_base(I_NO_NEXT) + H)
            sp.dma_start(w1_sb, t_in["We1"].rearrange("e d f -> d e f")).then_inc(experts_loaded, 16)
            for e in range(E):
                sp.dma_start(w2_sb[:, e, :, :], t_in["We2"][e].rearrange("(f p) d -> p f d", p=P)).then_inc(experts_loaded, 16)
            sp.dma_start(mem0[:, 8192:8832], t_in["routing"]).then_inc(experts_loaded, 16)
            sp.wait_ge(k_rot, 4 * B)
            sp.dma_start(xn_all[:, :, :].rearrange("p (b t) c -> p b (t c)", b=B),
                         xn_dram[:, :, :].rearrange("b p f -> p b f")).then_inc(xn_loaded, 16)
            ov = out.rearrange("b (t p) c -> p (b t) c", p=P)
            for b in range(B):
                sp.wait_ge(out_ready, b + 1)
                sp.dma_start(ov[:, b * NT:(b + 1) * NT, :], x_all[:, b * NT:(b + 1) * NT, :]).then_inc(out_stored, 16)
            sp.wait_ge(out_stored, 16 * B)

        @block.tensor
        def _(pe):
            def three(o, wh, wl, xh, xl, start=True, stop=True):
                pe.matmul(o, wh, xh, start=start, stop=False)
                pe.matmul(o, wh, xl, start=False, stop=False)
                return pe.matmul(o, wl, xh, start=False, stop=stop)

            def landed(kind, i, tasks, bank=None, place=0):
                most = {bank: place} if bank is not None else {}
                for name, n in tasks:
                    b, p = task_at(kind, name, n)
                    most[b] = max(most.get(b, 0), p)
                for b, p in sorted(most.items()):
                    if p or not (isinstance(i, int) and i == -1):
                        pe.wait_ge(m_done[b], task_base(i, b) + p)

            def task(kind, i, what, m, bank, place):
                o = ps_m[bank]
                reads = []
                if is_first(kind, ("q0", "k0", "v0"), what, m):
                    reads = [("xT0", 0)]
                elif is_first(kind, ("vT",), what, m):
                    reads = [("v1", n) for n in range(4)]
                elif what == "logit":
                    reads = [("xT1", 0)]
                landed(kind, i, reads, bank, place - 1)
                if kind == PRO and what in ("q0", "k0", "v0") and m == 0:
                    pe.wait_ge(w0_split, 1 + ("q0", "k0", "v0").index(what))
                if kind == FIRST and what == "proj0":
                    pe.wait_ge(wf_split, 2)
                    pe.wait_ge(const_loaded, 16 * N_CONST)
                if what == "xT0" or what == "xT1":
                    n = int(what == "xT1")
                    pe.wait_ge(xn_ready[n], ln_number(n, i) + 1)
                    src = xn1 if n else xn0
                    for t in range(NT):
                        last = pe.transpose(o[:, t * P:(t + 1) * P], src[:, t, :], ident[:, :])
                elif what in ("q0", "k0"):
                    w = 0 if what == "q0" else 1
                    for a in range(2):
                        col = slice((2 * m + a) * P, (2 * m + a + 1) * P)
                        last = three(o[:, a * T:(a + 1) * T], w0[:, 0, w, col], w0[:, 1, w, col],
                                     xT0[:, 0, :], xT0[:, 1, :])
                elif what == "v0":
                    t, f = m // 2, m % 2
                    tok, col = slice(t * P, (t + 1) * P), slice(f * 512, (f + 1) * 512)
                    last = three(o[:, :], xT0[:, 0, tok], xT0[:, 1, tok], w0[:, 0, 2, col], w0[:, 1, 2, col])
                elif what == "q1":
                    for a in range(2):
                        col = slice((2 * m + a) * P, (2 * m + a + 1) * P)
                        last = three(o[:, a * T:(a + 1) * T], wq1[:, 0, col], wq1[:, 1, col],
                                     xT1[:, 0, :], xT1[:, 1, :])
                elif what == "k1":
                    f, t = m // 2, m % 2
                    tok, col = slice(t * P, (t + 1) * P), slice(f * 512, (f + 1) * 512)
                    last = three(o[:, :], xT1[:, 0, tok], xT1[:, 1, tok], wkv1[:, 0, 0, col], wkv1[:, 1, 0, col])
                elif what == "v1":
                    for a in range(2):
                        col = slice((2 * m + a) * P, (2 * m + a + 1) * P)
                        last = three(o[:, a * T:(a + 1) * T], wkv1[:, 0, 1, col], wkv1[:, 1, 1, col],
                                     xT1[:, 0, :], xT1[:, 1, :])
                elif what == "kT":
                    pe.wait_ge(k_rot, (i - 1) * 4 + 2 * (m // 2) + 2)
                    for a in range(2):
                        c = (2 * m + a) % 4
                        for t in range(NT):
                            src = k_tok[:, t, c * P:(c + 1) * P]
                            last = pe.transpose(o[:, a * T + t * P:a * T + (t + 1) * P], src, ident[:, :])
                elif what == "vT":
                    for a in range(4):
                        last = pe.transpose(o[:, a * P:(a + 1) * P], v_col[:, 4 * m + a, :], ident[:, :])
                elif what == "proj0" or what == "proj1":
                    n_pairs = NJ if what == "proj0" or kind == LAST else 2 * NJ
                    pe.wait_ge(o_copied, pair_base(i) + n_pairs)
                    w = lin if what == "proj0" else wo
                    for t in range(NT):
                        tok = slice(t * P, (t + 1) * P)
                        for j in range(NJ):
                            last = pe.matmul(o[:, tok], oT[:, j, tok], w[:, j, :], start=(j == 0),
                                             stop=(what == "proj1" and j == NJ - 1))
                        if what == "proj0":
                            last = three(o[:, tok], xT0[:, 0, tok], xT0[:, 1, tok], we[:, 0, :], we[:, 1, :],
                                         start=False)
                elif what == "logit":
                    for t in range(NT):
                        tok = slice(t * P, (t + 1) * P)
                        last = three(o[:, t * E:(t + 1) * E], xT1[:, 0, tok], xT1[:, 1, tok],
                                     wg[:, 0, :], wg[:, 1, :])
                last.then_inc(m_ready[bank], 1)

            def scores(kind, i, k):
                o = ps_s[k % NS]
                a = heads_a(kind)
                if k >= NS:
                    pe.wait_ge(p_ready, head_base(i) + k - NS + 1)
                if k < a:
                    j, hh = k // 2, k % 2
                    if k == 0:
                        for n in range(2):
                            after = [tasks_in(x, n) - max(p for what, _, b, p in schedule(x) if b == n and what in ("q0", "k0", "v0"))
                                     for x in ([PRO] if kind == FIRST else [FIRST, FULL])]
                            pe.wait_ge(m_done[n], task_base(i, n) - min(after))
                    pe.matmul(o[:, 0:P], q_pad[:, j, hh, 0:P], k_pair[:, j, 0:P], start=True, stop=True)
                    last = pe.matmul(o[:, P:P + T], q_pad[:, j, hh, P:T], k_pair[:, j, :], start=True, stop=True)
                else:
                    h = k - a
                    if h == 0:
                        landed(kind, i, [t[1:] for t in QKV1 if t[1] in ("q1", "kT", "vT")])
                    for e in range(2):
                        last = pe.matmul(o[:, e * T:(e + 1) * T], q_rot[:, h, e, :, :].rearrange("p j t -> p (j t)"),
                                         k_dup[:, h, :, :, :].rearrange("p a j t -> p (a j t)"), start=True, stop=True)
                last.then_inc(s_ready, 1)

            def transposes(kind, i, k):
                o, src = ps_t[k % NPT], prob[:, k % NP_, :]
                pe.wait_ge(norm_ready, head_base(i) + k + 1)
                if k >= NPT:
                    pe.wait_ge(t_copied[k % 2], pair_base(i) + k // 2)
                if k < heads_a(kind):
                    blocks = [(0, 0), (1, 1), (2, 2)]
                else:
                    blocks = [(0, 0), (1, 2), (2, 1), (3, 3)]
                for dst, s in blocks:
                    last = pe.transpose(o[:, dst * P:(dst + 1) * P], src[:, s * P:(s + 1) * P], ident[:, :])
                last.then_inc(t_ready, 1)

            def outputs(kind, i, k):
                a = heads_a(kind)
                pt = probT[:, k % NPT, :]
                pe.wait_ge(t_copied[k % 2], pair_base(i) + k // 2 + 1)
                pair = k // 2
                if k % 2 == 0 and pair >= 1:
                    pe.wait_ge(o_copied, pair_base(i) + pair)
                o = ps_o[:, 0:T]
                if k < a:
                    j, hh = k // 2, k % 2
                    pe.matmul(o, v_pair[:, 0, j, hh:hh + 2, :].rearrange("p a d -> p (a d)"), pt[:, 0:T],
                              start=(hh == 0), stop=False)
                    last = pe.matmul(o[:, P:T], v_pair[:, 1, j, hh:hh + 2, :].rearrange("p a d -> p (a d)"), pt[:, T:384],
                                     start=False, stop=(hh == 1))
                else:
                    h = k - a
                    oh = o[:, (k % 2) * P:(k % 2 + 1) * P]
                    for kb in range(2):
                        at = P * (2 * h + kb)
                        for e in range(2):
                            w = v_row[:, at + 64:at + 64 + P] if e == 0 else v_row[:, at:at + P]
                            last = pe.matmul(oh, w, pt[:, (2 * kb + e) * P:(2 * kb + e + 1) * P],
                                             start=(kb == 0 and e == 0), stop=(kb == 1 and e == 1))
                last.then_inc(pv_done, 1)

            def iteration(kind, i):
                for what, m, bank, place in schedule(kind):
                    if what == "S":
                        scores(kind, i, m)
                    elif what == "T":
                        transposes(kind, i, m)
                    elif what == "PV":
                        outputs(kind, i, m)
                    elif what == "wf":
                        pe.wait_ge(thr_step, 1)
                        pe.wait_ge(zeroed, 4)
                        pe.wait_ge(m_done[0], tasks_in(PRO, 0))
                        pe.matmul(ps_m[0][:, 0:1], ones[:, :], thr[:, 0:1], start=True, stop=True).then_inc(abs_sum, 1)
                    elif bank is not None:
                        if kind == LAST and place == 1:
                            landed(kind, i, [], 1 - bank, 0)
                        task(kind, i, what, m, bank, place)

            pe.wait_ge(ident_loaded, 16)
            iteration(PRO, -1)
            pe.wait_ge(zeroed, 4)
            iteration(FIRST, 0)
            pe.wait_ge(w1_split, 8)
            with pe.Fori(I_LOOP, I_NO_NEXT) as i:
                iteration(FULL, i)
            iteration(NO_NEXT, I_NO_NEXT)
            iteration(LAST, I_LAST)

            pe.wait_ge(experts_loaded, 16 * (E + 2))
            pe.wait_ge(route, ROUTE_MASK)
            chosen = wide[5].rearrange("p (b t) e -> p b t e", t=NT)
            pe.matmul(ps_s[0][:, 0:B * E], upper, chosen[:, :, 0, :], start=True, stop=True)
            pe.matmul(ps_s[0][:, B * E:2 * B * E], upper, chosen[:, :, 1, :], start=True, stop=False)
            pe.matmul(ps_s[0][:, B * E:2 * B * E], ones[:, :], chosen[:, :, 0, :], start=False, stop=True).then_inc(pos_ready, 1)
            pe.wait_ge(xn_loaded, 16)
            for n in range(2):
                pe.wait_ge(t_copied[n], pair_base(I_LAST) + NJ)
                pe.wait_ge(m_done[n], task_base(I_LAST, n) + tasks_in(LAST, n))
            for b in range(B):
                pe.wait_ge(disp_ready, NT * (b + 1))
                bank = ps_t[b // 2 % 2]
                if b % 2 == 0 and b >= 4:
                    pe.wait_ge(xe_copied, b // 2 - 1)
                for t in range(NT):
                    last = pe.matmul(bank[:, (b % 2) * T:(b % 2 + 1) * T], xn_all[:, b * NT + t, :],
                                     disp[:, b * NT + t, :], start=(t == 0), stop=(t == NT - 1))
                if b % 2:
                    last.then_inc(xe_ready, 1)
                if b >= 2:
                    pe.wait_ge(dT_copied, b - 1)
                for g in range(2):
                    for t in range(NT):
                        last = pe.transpose(ps_m[b % 2][:, g * T + t * P:g * T + (t + 1) * P],
                                            disp[:, b * NT + t, g * P:(g + 1) * P], ident[:, :])
                last.then_inc(dT_ready, 1)

            def hidden(e):
                for f2 in range(2):
                    n = 2 * e + f2
                    if n >= NS:
                        pe.wait_ge(h_gelu, n - NS + 1)
                    for f in range(2):
                        col = slice((2 * f2 + f) * P, (2 * f2 + f + 1) * P)
                        last = pe.matmul(ps_s[n % NS][:, f * T:(f + 1) * T], w1_sb[:, e, col],
                                         xe[:, e, :, :].rearrange("p b s -> p (b s)"), start=True, stop=True)
                    last.then_inc(h_ready, 1)

            pe.wait_ge(xe_copied, B // 2)
            hidden(0)
            for e in range(E):
                if e + 1 < E:
                    hidden(e + 1)
                pe.wait_ge(h_gelu, 2 * e + 2)
                if e >= 2:
                    pe.wait_ge(y_copied, e - 1)
                for f in range(NF):
                    last = pe.matmul(ps_y[e % 2][:, 0:T], w2_sb[:, e, f, :], hid[e % 2][:, f * T:(f + 1) * T],
                                     start=(f == 0), stop=(f == NF - 1))
                last.then_inc(y_ready, 1)
            pe.wait_ge(y_copied, E)

            def turn(n):
                if n >= 2:
                    pe.wait_ge(ys_copied, n - 1)
                for b in range(2):
                    for g in range(2):
                        last = pe.transpose(ps_t[n % 2][:, (2 * b + g) * P:(2 * b + g + 1) * P],
                                            yT[:, 2 * n + b, 4 * g:4 * g + 4, :].rearrange("p e s -> p (e s)"), ident[:, :])
                last.then_inc(ys_ready, 1)

            pe.wait_ge(dT_copied, B)
            turn(0)
            for n in range(B // 2):
                if n + 1 < B // 2:
                    turn(n + 1)
                pe.wait_ge(ys_copied, n + 1)
                for b in (2 * n, 2 * n + 1):
                    if b >= 2:
                        pe.wait_ge(out_ready, b - 1)
                    for t in range(NT):
                        for g in range(2):
                            last = pe.matmul(ps_m[b % 2][:, t * P:(t + 1) * P], dT[:, b, g * T + t * P:g * T + (t + 1) * P],
                                             ys[:, b, g, :], start=(g == 0), stop=(g == 1))
                    last.then_inc(c_ready, 1)

        @block.vector
        def _(dve):
            def ln_stats(b, i):
                n = ln_number(b, i)
                rows = batch_rows(i if b else i + 1)
                dve.wait_ge(x_loaded[0 if isinstance(i, int) and i == -1 else 1], 16)
                if b:
                    wait_apart(dve, x1_step, i + 1)
                for t in range(NT):
                    dve.bn_stats(stats[:, b, t, :],
                                 x_all[:, bass.ds(rows + t, 1), :].rearrange("p a c -> p (a c)")).then_inc(ln_stat[b], 1)
                wait_apart(dve, ln_stat[b], n * NT + NT)
                for t in range(NT):
                    dve.bn_aggr(mv[:, b, t, :], stats[:, b, t, :]).then_inc(ln_mv[b], 1)

            def ln_apply(b, i):
                n = ln_number(b, i)
                rows = batch_rows(i if b else i + 1)
                dst = xn1 if b else xn0
                dve.wait_ge(ln_rstd[b], n + 1)
                if b and not (isinstance(i, int) and i == 0):
                    dve.wait_ge(xn_saved, i * 16)
                for t in range(NT):
                    ins = dve.tensor_scalar(dst[:, t, :], x_all[:, bass.ds(rows + t, 1), :].rearrange("p a c -> p (a c)"),
                                            mv[:, b, t, 0:1], rstd[:, b, t:t + 1], ALU.subtract, ALU.mult)
                ins.then_inc(xn_ready[b], 1)

            def task(kind, i, what, m, bank, place):
                if what in ("q0", "v1", "vT"):
                    return
                o = ps_m[bank]
                dve.wait_ge(m_ready[bank], task_base(i, bank) + place)
                if kind == FIRST and what == "proj0":
                    dve.wait_ge(const_loaded, 16 * N_CONST)
                if what == "xT0" or what == "xT1":
                    n = int(what == "xT1")
                    dve.wait_ge(xt_hi[n], ln_number(n, i) + 1)
                    dst = xT0 if what == "xT0" else xT1
                    ins = dve.tensor_tensor(dst[:, 1, :], o[:, 0:T], dst[:, 0, :].bitcast(F32), ALU.subtract)
                elif what == "k0":
                    ins = dve.tensor_copy(k_pair[:, 2 * m:2 * m + 2, :].rearrange("p j t -> p (j t)"), o[:, :])
                elif what == "v0":
                    t, f = m // 2, m % 2
                    ins = dve.tensor_copy(v_pair[:, t, 4 * f:4 * f + 4, 0:3:2, :],
                                          o[:, :].rearrange("p (j a d) -> p j a d", j=4, a=2))
                elif what == "q1":
                    ins = dve.tensor_tensor(q_rot[:, :, :, m, :].rearrange("p h a t -> p a h t"),
                                            o[:, :].rearrange("p (a h t) -> p a h t", a=2, h=H),
                                            rope_q[:, m, :, :].unsqueeze(2).broadcast_to([P, 2, H, TPH]), ALU.mult)
                elif what == "kT":
                    ins = turned_k(dve, kind, i, o, m, 1)
                elif what == "k1":
                    f, t = m // 2, m % 2
                    if m:
                        dve.wait_ge(k_rot, (i - 1) * 4 + m)
                    dve.tensor_tensor(k_cos.rearrange("p (a b) -> p a b", b=2),
                                      o[:, :].rearrange("p (a b) -> p a b", b=2),
                                      cos_k[:, f * 256:(f + 1) * 256].unsqueeze(2).broadcast_to([P, 256, 2]), ALU.mult)
                    s = sin_k[:, f * 256:(f + 1) * 256]
                    d = k_sin.rearrange("p (a b) -> p a b", b=2)
                    ov = o[:, :].rearrange("p (a b) -> p a b", b=2)
                    dve.scalar_tensor_tensor(d[:, :, 0], ov[:, :, 1], -1.0, s, ALU.mult, ALU.mult)
                    ins = dve.tensor_tensor(d[:, :, 1], ov[:, :, 0], s, ALU.mult)
                elif what == "proj0":
                    rows = x_all[:, bass.ds(batch_rows(i), NT), :]
                    ins = dve.tensor_tensor(rows, o[:, 0:NT * C].rearrange("p (t c) -> p t c", t=NT), rows, ALU.add)
                    ins.then_inc(m_done[bank], 1)
                    dve.wait_ge(m_done[bank], task_base(i, bank) + place)
                    ins = dve.tensor_tensor(rows, rows, bias[:, :].unsqueeze(1).broadcast_to([P, NT, C]), ALU.add)
                    ins.then_inc(x1_step, 1)
                    return
                elif what == "proj1":
                    rows = x_all[:, bass.ds(batch_rows(i - 1), NT), :]
                    ins = dve.tensor_tensor(rows, o[:, 0:NT * C].rearrange("p (t c) -> p t c", t=NT), rows, ALU.add)
                elif what == "logit":
                    ins = dve.tensor_copy(lg_all[:, bass.ds(batch_rows(i), NT), :],
                                          o[:, 0:NT * E].rearrange("p (t e) -> p t e", t=NT))
                ins.then_inc(m_done[bank], 1)

            def ternary_weight():
                dve.wait_ge(wf_loaded[1], 32)
                dve.wait_ge(abs_sum, 1)
                dve.tensor_scalar(thr[:, 1:2], ps_m[0][:, 0:1], THRESH / (C * C), None, ALU.mult).then_inc(thr_step, 1)
                dve.wait_ge(thr_step, 2)
                dve.tensor_scalar(thr[:, 2:3], thr[:, 1:2], -1.0, None, ALU.mult).then_inc(thr_step, 1)
                dve.tensor_scalar(wf_above, wf_raw, thr[:, 1:2], None, ALU.is_gt).then_inc(thr_step, 1)
                dve.wait_ge(thr_step, 4)
                dve.scalar_tensor_tensor(we_sign, wf_raw, thr[:, 2:3], wf_above, ALU.is_lt, ALU.subtract).then_inc(thr_step, 1)
                dve.wait_ge(thr_step, 5)
                dve.tensor_scalar(we_full, we_sign, alpha[:, 0:1], -1.0, ALU.mult, ALU.mult).then_inc(thr_step, 1)
                dve.wait_ge(thr_step, 6)
                dve.tensor_copy(we[:, 0, :], we_full).then_inc(thr_step, 1)
                dve.tensor_copy(wg[:, 0, :], wg_raw).then_inc(thr_step, 1)
                dve.wait_ge(thr_step, 8)
                dve.tensor_tensor(we[:, 1, :], we_full, we[:, 0, :].bitcast(F32), ALU.subtract).then_inc(wf_split, 1)
                dve.tensor_tensor(wg[:, 1, :], wg_raw, wg[:, 0, :].bitcast(F32), ALU.subtract).then_inc(wf_split, 1)

            def maxima(kind, i, k):
                o, nm = ps_s[k % NS], nmax[:, k % NS, :]
                if kind == FIRST and k == 0:
                    dve.wait_ge(mask_loaded, 16)
                wait_apart(dve, s_ready, head_base(i) + k + 1)
                if k < heads_a(kind):
                    dve.tensor_tensor_reduce(o[:, 0:P], o[:, 0:P], mask[:, P:T], -1.0, BIG, ALU.add, ALU.min, nm[:, 0:1])
                    ins = dve.tensor_tensor_reduce(o[:, P:384], o[:, P:384], mask[:, :], -1.0, BIG, ALU.add,
                                                   ALU.min, nm[:, 1:2])
                else:
                    ins = dve.tensor_reduce(nm, o[:, :].rearrange("p (a t) -> p a t", a=2), AX.X, ALU.max, negate=True)
                ins.then_inc(max_ready, 1)

            def iteration(kind, i):
                for what, m, bank, place in schedule(kind):
                    if what == "S":
                        maxima(kind, i, m)
                    elif what == "R":
                        dve.wait_ge(p_ready, head_base(i) + m + 1)
                        dve.reciprocal(rinv[:, m % NS, :], rsum[:, m % NS, :]).then_inc(rinv_ready, 1)
                    elif what == "T" and m % 2 == 1:
                        dve.wait_ge(t_ready, head_base(i) + m + 1)
                        if m >= NPT:
                            dve.wait_ge(pv_done, head_base(i) + m - NPT + 1)
                        n = 384 if m < heads_a(kind) else 512
                        dve.tensor_copy(probT[:, m % NPT, 0:n], ps_t[m % NPT][:, 0:n]).then_inc(t_copied[1], 1)
                    elif what == "stat":
                        ln_stats(m, i)
                    elif what == "norm":
                        ln_apply(m, i)
                    elif what == "zeros":
                        dve.memset(ones[:, :], 1.0).then_inc(zeroed, 1)
                        dve.memset(v_pair[:, :, :, 1, :], 0.0).then_inc(zeroed, 1)
                    elif what == "wf":
                        ternary_weight()
                    elif what == "w0":
                        dve.wait_ge(w0_hi, m + 1)
                        dve.tensor_tensor(w0[:, 1, m, :], q_flat[:, m * HD:(m + 1) * HD], w0[:, 0, m, :].bitcast(F32),
                                          ALU.subtract).then_inc(w0_split, 1)
                    elif what == "w1lo":
                        dve.wait_ge(w1_hi, m + 1)
                        dve.tensor_tensor(w1_part(m, 1), k_flat[:, m * 512:(m + 1) * 512], w1_part(m, 0).bitcast(F32),
                                          ALU.subtract).then_inc(w1_split, 1)
                    elif bank is not None:
                        task(kind, i, what, m, bank, place)

            dve.memset(half_pow[:, :], -0.5).then_inc(zeroed, 1)
            dve.memset(q_pad[0:DK, :, 1, :], 0.0).then_inc(zeroed, 1)
            dve.wait_ge(wf_loaded[0], 16)
            dve.tensor_reduce(thr[:, 0:1], wf_raw, AX.X, ALU.add, apply_absolute_value=True).then_inc(thr_step, 1)
            iteration(PRO, -1)
            iteration(FIRST, 0)
            with dve.Fori(I_LOOP, I_NO_NEXT) as i:
                iteration(FULL, i)
            iteration(NO_NEXT, I_NO_NEXT)
            iteration(LAST, I_LAST)

            steps = [0]

            def then(ins):
                steps[0] += 1
                ins.then_inc(route, 1)
                dve.wait_ge(route, steps[0])

            def wider(a):
                return a.unsqueeze(2).broadcast_to([P, B * NT, E])

            top, total, inv, gate, best, pos, off, keep, slot = thin[0:9]
            logits = lg_all[:, :, :]
            dve.wait_ge(experts_loaded, 16 * (E + 2))
            then(dve.tensor_reduce(top, logits, AX.X, ALU.max))
            then(dve.tensor_tensor(wide[0], logits, wider(top), ALU.subtract))
            dve.wait_ge(route_exp, 1)
            then(dve.tensor_reduce(total, wide[1], AX.X, ALU.add))
            then(dve.reciprocal(inv, total))
            then(dve.tensor_tensor(wide[2], wide[1], wider(inv), ALU.mult))
            then(dve.tensor_reduce(gate, wide[2], AX.X, ALU.max))
            then(dve.tensor_tensor(wide[3], wide[2], wider(gate), ALU.is_equal))
            then(dve.tensor_tensor(wide[4], wide[3], rank, ALU.mult))
            then(dve.tensor_reduce(best, wide[4], AX.X, ALU.max))
            then(dve.tensor_tensor(wide[5], wide[4], wider(best), ALU.is_equal))
            assert steps[0] == ROUTE_MASK
            then(dve.tensor_tensor(wide[7], wide[5], first_slot, ALU.mult))
            then(dve.tensor_reduce(off, wide[7], AX.X, ALU.add))
            dve.wait_ge(pos_ready, 1)
            then(dve.tensor_tensor(wide[6].rearrange("p (b t) e -> p t b e", t=NT),
                                   ps_s[0][:, 0:2 * B * E].rearrange("p (t b e) -> p t b e", t=NT, b=B),
                                   wide[5].rearrange("p (b t) e -> p t b e", t=NT), ALU.mult))
            then(dve.tensor_reduce(pos, wide[6], AX.X, ALU.add))
            then(dve.tensor_scalar(keep, pos, float(CAP), None, ALU.is_lt))
            then(dve.tensor_tensor(slot, pos, off, ALU.add))
            then(dve.scalar_tensor_tensor(slot, slot, 1.0, keep, ALU.add, ALU.mult))
            then(dve.tensor_scalar(slot, slot, -1.0, None, ALU.add))
            for n in range(B * NT):
                dve.tensor_scalar(disp[:, n, :], iota, slot[:, n:n + 1], None, ALU.is_equal).then_inc(disp_ready, 1)
            for b in range(B):
                dve.wait_ge(dT_ready, b + 1)
                dve.tensor_copy(dT[:, b, :], ps_m[b % 2][:, :]).then_inc(dT_copied, 1)
            for e in range(E):
                dve.wait_ge(y_ready, e + 1)
                dve.tensor_copy(yT[:, :, e, :], ps_y[e % 2][:, 0:T].rearrange("p (b s) -> p b s", b=B)).then_inc(y_copied, 1)
            for b in range(B):
                dve.wait_ge(c_ready, b + 1)
                for t in range(NT):
                    n = b * NT + t
                    ins = dve.scalar_tensor_tensor(x_all[:, n, :], ps_m[b % 2][:, t * P:(t + 1) * P], gate[:, n:n + 1],
                                                   x_all[:, n, :], ALU.mult, ALU.add)
                ins.then_inc(out_ready, 1)

        @block.scalar
        def _(act):
            def task(kind, i, what, m, bank, place):
                o = ps_m[bank]
                if what not in ("xT0", "xT1", "q0", "kT", "v1", "vT"):
                    return
                act.wait_ge(m_ready[bank], task_base(i, bank) + place)
                if what == "xT0" or what == "xT1":
                    dst = xT0 if what == "xT0" else xT1
                    act.activation(dst[:, 0, :], o[:, 0:T], ACT.Copy).then_inc(xt_hi[int(what == "xT1")], 1)
                    return
                if what == "q0":
                    if kind == PRO and m == 0:
                        act.wait_ge(zeroed, 2)
                        act.wait_ge(pool_zeroed, 1)
                    for hh in range(2):
                        rows = slice(hh * DK, (hh + 1) * DK)
                        ins = act.activation(q_pad[rows, 2 * m:2 * m + 2, hh, :],
                                             o[rows, :].rearrange("p (j t) -> p j t", j=2), ACT.Copy, scale=float(DK) ** 0.5)
                elif what == "kT":
                    turned_k(act, kind, i, o, m, 0)
                    return
                elif what == "v1":
                    ins = act.activation(v_col[:, :, 2 * m * TPH:(2 * m + 2) * TPH].rearrange("p h (j t) -> p j h t", j=2),
                                         o[:, :].rearrange("p (j h t) -> p j h t", j=2, h=H), ACT.Copy)
                elif what == "vT":
                    if is_first(kind, ("vT",), what, m):
                        act.wait_ge(pool_zeroed, 2)
                    ins = act.activation(v_row[:, 64 + 8 * P * m:64 + 8 * P * (m + 1)].rearrange("p (a d) -> p a d", d=P)[:, :, 0:DK],
                                         o[:, :].rearrange("p (a d) -> p a d", d=DK), ACT.Copy)
                ins.then_inc(m_done[bank], 1)

            def exps(kind, i, k):
                o, nm, rs = ps_s[k % NS], nmax[:, k % NS, :], rsum[:, k % NS, :]
                p = prob[:, k % NP_, :]
                act.wait_ge(max_ready, head_base(i) + k + 1)
                if k >= NP_:
                    act.wait_ge(t_ready, head_base(i) + k - NP_ + 1)
                if k < heads_a(kind):
                    parts, scale = [(0, P), (P, 384)], -1.0
                else:
                    parts, scale = [(0, T), (T, 2 * T)], 1.0
                for n, (lo, hi) in enumerate(parts):
                    ins = act.activation(p[:, lo:hi], o[:, lo:hi], ACT.Exp, bias=nm[:, n:n + 1], scale=scale,
                                         accum_out=rs[:, n:n + 1])
                ins.then_inc(p_ready, 1)

            def iteration(kind, i):
                for what, m, bank, place in schedule(kind):
                    if what == "S":
                        exps(kind, i, m)
                    elif what == "T" and m % 2 == 0:
                        act.wait_ge(t_ready, head_base(i) + m + 1)
                        if m >= NPT:
                            act.wait_ge(pv_done, head_base(i) + m - NPT + 1)
                        n = 384 if m < heads_a(kind) else 512
                        act.activation(probT[:, m % NPT, 0:n], ps_t[m % NPT][:, 0:n], ACT.Copy).then_inc(t_copied[0], 1)
                    elif what == "w0":
                        act.wait_ge(w0_loaded[m], 16)
                        act.activation(w0[:, 0, m, :], q_flat[:, m * HD:(m + 1) * HD], ACT.Copy).then_inc(w0_hi, 1)
                    elif what == "w1hi":
                        act.wait_ge(w1_loaded, 16)
                        act.activation(w1_part(m, 0), k_flat[:, m * 512:(m + 1) * 512], ACT.Copy).then_inc(w1_hi, 1)
                    elif what == "O":
                        act.wait_ge(pv_done, head_base(i) + 2 * m + 2)
                        src, p2 = ps_o[:, 0:T], m % NJ
                        if 2 * m < heads_a(kind):
                            ins = act.activation(oT[:, p2, :], src, ACT.Copy)
                        else:
                            ins = act.activation(oT[:, :, 2 * p2 * TPH:(2 * p2 + 2) * TPH].rearrange("p j (h t) -> p h j t", h=2),
                                                 src.rearrange("p (h j t) -> p h j t", h=2, j=NJ), ACT.Copy)
                        ins.then_inc(o_copied, 1)
                    elif bank is not None:
                        task(kind, i, what, m, bank, place)

            iteration(PRO, -1)
            iteration(FIRST, 0)
            with act.Fori(I_LOOP, I_NO_NEXT) as i:
                iteration(FULL, i)
            iteration(NO_NEXT, I_NO_NEXT)
            iteration(LAST, I_LAST)

            act.wait_ge(route, 2)
            act.activation(wide[1], wide[0], ACT.Exp).then_inc(route_exp, 1)
            for n in range(B // 2):
                act.wait_ge(xe_ready, n + 1)
                act.activation(xe[:, :, 2 * n:2 * n + 2, :].rearrange("p e b s -> p b e s"),
                               ps_t[n % 2][:, :].rearrange("p (b e s) -> p b e s", b=2, e=E), ACT.Copy).then_inc(xe_copied, 1)
            for n in range(2 * E):
                act.wait_ge(h_ready, n + 1)
                e, f2 = n // 2, n % 2
                if e >= 2:
                    act.wait_ge(y_ready, e - 1)
                act.activation(hid[e % 2][:, f2 * 512:(f2 + 1) * 512], ps_s[n % NS][:, :], ACT.Gelu_apprx_tanh).then_inc(h_gelu, 1)
            for n in range(B // 2):
                act.wait_ge(ys_ready, n + 1)
                act.activation(ys[:, 2 * n:2 * n + 2, :, :].rearrange("p b g d -> p (b g d)"), ps_t[n % 2][:, :],
                               ACT.Copy).then_inc(ys_copied, 1)

        @block.gpsimd
        def _(pool):
            def iteration(kind, i):
                for what, m, bank, place in schedule(kind):
                    if what == "R":
                        p, r = prob[:, m % NP_, :], rinv[:, m % NS, :]
                        pool.wait_ge(rinv_ready, head_base(i) + m + 1)
                        if m < heads_a(kind):
                            pool.tensor_tensor(p[:, 0:P], p[:, 0:P], r[:, 0:1].broadcast_to([P, P]), ALU.mult)
                            ins = pool.tensor_tensor(p[:, P:384], p[:, P:384], r[:, 1:2].broadcast_to([P, T]), ALU.mult)
                        else:
                            pv = p.rearrange("p (a t) -> p a t", a=2)
                            ins = pool.tensor_tensor(pv, pv, r.unsqueeze(2).broadcast_to([P, 2, T]), ALU.mult)
                        ins.then_inc(norm_ready, 1)
                    elif what == "stat":
                        n = ln_number(m, i)
                        wait_apart(pool, ln_mv[m], n * NT + NT)
                        pool.tensor_scalar(vareps[:, m, :], mv[:, m, :, 1], EPS, None, ALU.add).then_inc(ln_eps[m], 1)
                        pool.wait_ge(ln_eps[m], n + 1)
                        pool.tensor_tensor(rstd[:, m, :], vareps[:, m, :], half_pow[:, :], ALU.pow).then_inc(ln_rstd[m], 1)
                    elif what == "k1":
                        t = m % 2
                        pool.wait_ge(m_done[bank], task_base(i, bank) + place)
                        pool.tensor_tensor(k_tok[:, t, :], k_cos, k_sin, ALU.add).then_inc(k_rot, 1)

            pool.wait_ge(zeroed, 1)
            iteration(PRO, -1)
            pool.wait_ge(ln_rstd[0], 1)
            pool.memset(q_pad[DK:P, :, 0, :], 0.0).then_inc(pool_zeroed, 1)
            pool.wait_ge(pool_zeroed, 1)
            pool.memset(v_row[:, :], 0.0).then_inc(pool_zeroed, 1)
            iteration(FIRST, 0)
            with pool.Fori(I_LOOP, I_NO_NEXT) as i:
                iteration(FULL, i)
            iteration(NO_NEXT, I_NO_NEXT)
            iteration(LAST, I_LAST)


_INS = ["x", "w0", "w1", "wf", "wg", "alpha", "bias", "lin", "wo", "We1", "We2",
        "ident", "mask", "rope_q", "cos_k", "sin_k", "routing"]


def constants():
    inv = 1.0 / 10000.0 ** (np.arange(0, DK, 2, dtype=np.float32) / DK)
    ang = np.outer(np.arange(T, dtype=np.float32), inv.astype(np.float32))
    cos = np.ones((T, DK // 2), np.float32)
    sin = np.zeros((T, DK // 2), np.float32)
    cos[1:], sin[1:] = np.cos(ang[:T - 1]), np.sin(ang[:T - 1])
    pos = np.arange(T).reshape(TPH, H)
    signed = np.stack([-sin, sin], -1).reshape(T, DK)
    both = np.concatenate([np.repeat(cos, 2, 1), signed], 1) / np.float32(DK ** 0.5)
    rope_q = both[pos.T.reshape(NJ, 2, TPH)].transpose(3, 0, 1, 2).reshape(P, T)
    rows = pos[np.arange(P) % TPH]
    cos_k, sin_k = cos[rows].reshape(P, HD // 2), sin[rows].reshape(P, HD // 2)
    q, k = np.arange(P)[:, None], np.arange(T)[None, :]
    mask = np.where(k > q + P, NEG, 0)
    upper = (np.arange(P)[:, None] < np.arange(P)[None, :])
    iota = np.tile(np.arange(E * CAP), (P, 1))
    first = np.tile(np.arange(E) * CAP, (P, B * NT))
    rank = np.tile(E - np.arange(E), (P, B * NT))
    routing = np.concatenate([upper, iota, first, rank], 1)
    return {n: np.ascontiguousarray(a, np.float32) for n, a in dict(
        ident=np.eye(P), mask=mask, rope_q=rope_q, cos_k=cos_k, sin_k=sin_k, routing=routing).items()}


def laid_out(a):
    rows = lambda w: np.asarray(w).reshape(C, HD)
    cols = lambda w: np.asarray(w).T
    q1 = cols(a["L1_attn_wq"]).reshape(C, H, 1, DK // 2, 2)
    q1 = np.concatenate([q1, q1[..., ::-1]], 2).reshape(C, 2 * HD)
    d = dict(
        x=a["L0_attn_x"],
        w0=np.concatenate([rows(a["L0_attn_query_mat"]), rows(a["L0_attn_key_mat"]), rows(a["L0_attn_value_mat"])], 1),
        w1=np.concatenate([q1, cols(a["L1_attn_wk"]), cols(a["L1_attn_wv"])], 1),
        wf=cols(a["L0_ffn_weight"]), wg=a["L1_ffn_Wg"],
        alpha=np.broadcast_to(np.asarray(a["L0_ffn_alpha"]), (P, 1)),
        bias=np.broadcast_to(np.asarray(a["L0_ffn_bias"]), (P, C)),
        lin=a["L0_attn_linear_m1"], wo=cols(a["L1_attn_wo"]), We1=a["L1_ffn_W1"], We2=a["L1_ffn_W2"])
    d.update(constants())
    return {n: np.ascontiguousarray(d[n]) for n in _INS}


def kernel(**inputs):
    import concourse.bacc as bacc
    from concourse.bass_utils import run_bass_kernel_spmd as run

    nc = bacc.Bacc("TRN2", target_bir_lowering=False, num_devices=1)
    arrays, aps = {}, {}
    for name, a in laid_out(inputs).items():
        arrays[f"in_{name}_dram"] = a
        aps[name] = nc.dram_tensor(f"in_{name}_dram", a.shape, mybir.dt.from_np(a.dtype), kind="ExternalInput").ap()
    out = nc.dram_tensor("out_0_dram", (B, T, C), F32, kind="ExternalOutput").ap()
    build(nc, aps, out)
    r = run(nc, [arrays], core_ids=[0])
    return r.results[0]["out_0_dram"]
```

```python
from contextlib import ExitStack

import numpy as np

import concourse.bass as bass
from concourse import mybir

P = 128
B, T, C = 8, 256, 128
H, DK = 16, 64
HD = H * DK
NT = T // P
NJ = H // 2
TPH = T // H
E, FF, CAP = 8, 512, T // 8
NF = FF // P
EPS = 1e-5
ROUTING = P + E * CAP + 2 * B * NT * E
N_CONST = 6
THRESH = 0.7
NEG = -1.0e30
BIG = 3.0e38

F32 = mybir.dt.float32
F32R = mybir.dt.float32r
ALU = mybir.AluOpType
ACT = mybir.ActivationFunctionType
AX = mybir.AxisListType

NS, NP_, NPT = 3, 3, 2

ROUTE_MASK = 10

PRO, FIRST, FULL, NO_NEXT, LAST = range(5)
I_LOOP, I_NO_NEXT, I_LAST = 1, B - 1, B

QKV1 = [(0, "v1", 0), (1.5, "v1", 1), (2, "v1", 2), (2.5, "v1", 3), (3, "vT", 1), (3.5, "vT", 2), (4, "vT", 3),
        (5, "vT", 0), (5, "k1", 0), (6, "k1", 1), (6, "q1", 3), (8, "q1", 2), (8, "kT", 0), (9, "q1", 7),
        (9.5, "kT", 1), (10, "q1", 5), (10.5, "q1", 1), (11, "k1", 2), (12, "k1", 3), (13, "q1", 6), (14, "q1", 0),
        (14, "q1", 4), (14, "kT", 2), (14, "kT", 3)]
A_TASKS = [(4, "stat", 0), (20, "proj0", 0), (20.5, "norm", 0), (21, "stat", 1), (21.5, "xT0", 0), (29.5, "norm", 1),
           (33.5, "xT1", 0), (38, "logit", 0)]
QKV0 = [(22.5, "v0", 2), (24, "k0", 2), (26, "v0", 1), (27, "q0", 0), (27.5, "k0", 0), (29, "k0", 3), (31, "q0", 3),
        (32, "k0", 1), (32.5, "v0", 3), (33, "q0", 2), (33.5, "v0", 0), (34.5, "q0", 1)]
PRO_TASKS = [("stat", 0), ("zeros", 0), ("norm", 0), ("w0", 0), ("xT0", 0), ("w0", 1), ("w0", 2), ("q0", 0), ("k0", 0), ("v0", 0),
             ("q0", 1), ("k0", 1), ("v0", 1), ("q0", 2), ("k0", 2), ("v0", 2), ("q0", 3), ("k0", 3), ("v0", 3)]
NO_NEXT_TASKS = [(20, "proj0", 0), (20.5, "stat", 1), (21.5, "norm", 1), (22.5, "xT1", 0), (24, "v1z", 0),
                 (24, "v1z", 1), (24.5, "k1z", 0), (25, "v1z", 2), (25.5, "k1z", 1), (26, "v1z", 3), (26.5, "q1z", 0),
                 (27.5, "kTz", 0), (28, "q1z", 1), (28.5, "kTz", 1), (29, "k1z", 2), (29.5, "q1z", 2),
                 (30.5, "q1z", 3), (31, "k1z", 3), (31.5, "q1z", 4), (32.5, "q1z", 5), (33, "kTz", 2),
                 (33.5, "kTz", 3), (34, "q1z", 6), (34.5, "logit", 0), (35, "q1z", 7)]
LAST_TASKS = [(0, "vT", 0), (0.5, "vT", 1), (0.5, "route", 0), (1.5, "vT", 2), (1.5, "vT", 3), (1.5, "route", 1),
              (2.5, "route", 2), (3.5, "place", 0), (4.5, "route", 3), (5, "split", 0), (5.5, "slots", 0),
              (6, "split", 1), (7, "split", 2), (7, "slots", 1), (8, "dT", 0), (8, "split", 3), (9, "dT", 1),
              (9.5, "slots", 2), (9.5, "xe", 0), (10, "slots", 3), (10.5, "dT", 2), (11.5, "slots", 4),
              (11.5, "xe", 1), (11.5, "slots", 5), (12, "dT", 3), (13, "dT", 4), (13.5, "slots", 6), (13.5, "dT", 5),
              (14.5, "xe", 2), (15, "slots", 7), (16, "xe", 3), (16.5, "dT", 6), (17, "dT", 7)]
FIRST_TASKS = [(3.5, "w1hi", 0), (4.5, "w1hi", 1), (4.5, "w1lo", 0), (5.5, "w1hi", 2), (5.5, "w1lo", 1),
               (6.5, "w1hi", 3), (6.5, "w1lo", 2), (7.5, "w1hi", 4), (7.5, "w1lo", 3), (8.5, "w1hi", 5),
               (8.5, "w1lo", 4), (9.5, "w1hi", 6), (9.5, "w1lo", 5), (10.5, "w1hi", 7), (10.5, "w1lo", 6),
               (11.5, "w1lo", 7), (12, "stat", 0), (13, "norm", 0), (18.5, "wf", 0), (20, "proj0", 0), (20, "xT0", 0),
               (20, "q0", 0), (20, "k0", 0), (20, "stat", 1), (20, "v0", 0), (20, "q0", 1), (20, "k0", 1),
               (20, "norm", 1), (20, "v0", 1), (20, "q0", 2), (20, "k0", 2), (20, "v0", 2), (20, "q0", 3),
               (20, "k0", 3), (20, "v0", 3), (20, "xT1", 0), (20, "logit", 0)]


def schedule(kind):
    a = H if kind in (FIRST, FULL, NO_NEXT) else 0
    b = H if kind in (FULL, NO_NEXT, LAST) else 0
    n = a + b
    tasks = []
    if kind == PRO:
        tasks += [(0, *t) for t in PRO_TASKS]
    if kind == LAST:
        tasks += LAST_TASKS
    if kind in (FULL, NO_NEXT):
        tasks += QKV1
    if kind == FIRST:
        tasks += FIRST_TASKS
    elif kind == NO_NEXT:
        tasks += NO_NEXT_TASKS
    elif a:
        tasks += A_TASKS
    if kind == FULL:
        tasks += QKV0
    if b:
        tasks.append((n + 3.5, "proj1", 0))
    out = []
    for s in range(int(min(0, tasks[0][0])), int(max([t[0] for t in tasks] + [n + 3 if n else 0])) + 1):
        if 0 <= s < n:
            out.append(("S", s))
        if 0 <= s - 1 < n:
            out.append(("R", s - 1))
        out += [t[1:] for t in tasks if t[0] == s]
        if 0 <= s - 2 < n:
            out.append(("T", s - 2))
        if 0 <= s - 3 < n:
            out.append(("PV", s - 3))
            if (s - 3) % 2:
                out.append(("O", (s - 3) // 2))
        out += [t[1:] for t in tasks if t[0] == s + 0.5]
    assert all(t[1:] in out for t in tasks)
    done, placed = [0, 0], []
    for what, m in out:
        if what in TASKS:
            bank = sum(done) % 2
            done[bank] += 1
            placed.append((what, m, bank, done[bank]))
        else:
            placed.append((what, m, None, None))
    return placed


TASKS = ("xT0", "q0", "k0", "v0", "proj0", "xT1", "logit", "q1", "k1", "kT", "v1", "vT", "proj1", "q1z", "k1z", "kTz",
         "v1z", "place", "xe", "dT")


def tasks_in(kind, bank):
    return sum(1 for x in schedule(kind) if x[2] == bank)


def task_base(i, bank):
    if isinstance(i, int) and i < 1:
        return 0 if i == -1 else tasks_in(PRO, bank)
    before = tasks_in(PRO, bank) + tasks_in(FIRST, bank)
    if isinstance(i, int) and i == I_LAST:
        return before + (I_NO_NEXT - 1) * tasks_in(FULL, bank) + tasks_in(NO_NEXT, bank)
    return (i - 1) * tasks_in(FULL, bank) + before


def head_base(i):
    return 0 if isinstance(i, int) and i < 1 else i * (2 * H) - H


def pair_base(i):
    return 0 if isinstance(i, int) and i < 1 else i * H - NJ


def batch_rows(i):
    return i * NT


def heads_a(kind):
    return 0 if kind in (PRO, LAST) else H


def task_at(kind, name, m):
    for what, n, bank, place in schedule(kind):
        if (what, n) == (name, m):
            return bank, place
    raise ValueError((kind, name, m))


def order(name, kind):
    return [x[1] for x in schedule(kind) if x[0] == name]


def is_first(kind, names, what, m):
    return what in names and (what, m) == [x[:2] for x in schedule(kind) if x[0] in names][0]


def build(nc, t_in, out):
    ctx = ExitStack()
    with ctx:
        def sb(name, shape, dt=F32):
            return ctx.enter_context(nc.sbuf_tensor(name, shape, dt))

        def sem(name):
            return ctx.enter_context(nc.semaphore(name))

        w0 = sb("w0", [P, 2, 3, HD], F32R)
        wq1 = sb("wq1", [P, 2, 2 * HD], F32R)
        wkv1 = sb("wkv1", [P, 2, 2, HD], F32R)
        we = sb("we", [P, 2, C], F32R)
        wg = sb("wg", [P, 2, E], F32R)
        lin = sb("lin", [P, NJ, C])
        wo = sb("wo", [P, NJ, C])
        mem0 = sb("mem0", [P, 4096 + 2048 + 3072])
        q_pad = mem0[:, 0:4096].rearrange("p (j a t) -> p j a t", j=NJ, a=2)
        k_pair = mem0[:, 4096:6144].rearrange("p (j t) -> p j t", j=NJ)
        v_pair = mem0[:, 6144:9216].rearrange("p (b j a d) -> p b j a d", b=NT, j=NJ, a=3)
        q_rot = sb("q_rot", [P, H, 2, NJ, TPH])
        k_dup = sb("k_dup", [P, H, 2, NJ, TPH])
        q_flat = q_rot[:, :, :, :, :].rearrange("p h a j t -> p (h a j t)")
        k_flat = k_dup[:, :, :, :, :].rearrange("p h a j t -> p (h a j t)")
        q_last = mem0[:, 0:4096].rearrange("p (h a j t) -> p h a j t", h=H, a=2, j=NJ)
        k_last = mem0[:, 4096:8192].rearrange("p (h a j t) -> p h a j t", h=H, a=2, j=NJ)
        v_row = sb("v_row", [P, 64 + 2 * H * P])
        v_col = sb("v_col", [P, H, P])
        k_tok = sb("k_tok", [P, NT, HD // 2])
        wf_raw, we_sign, we_full, wf_above = [k_tok[:, 0, n * C:(n + 1) * C] for n in range(4)]
        wg_raw = k_tok[:, 1, 0:E]
        k_cos = v_col[:, 0:4, :].rearrange("p a b -> p (a b)")
        k_sin = v_col[:, 4:8, :].rearrange("p a b -> p (a b)")
        k_cos_last, k_sin_last = mem0[:, 8192:8704], mem0[:, 8704:9216]
        x_all = sb("x_all", [P, B * NT, C])
        lg_all = sb("lg_all", [P, B * NT, E])
        xn0 = sb("xn0", [P, NT, C])
        xn1 = sb("xn1", [P, NT, C])
        xT0 = sb("xT0", [P, 2, T], F32R)
        xT1 = sb("xT1", [P, 2, T], F32R)
        prob = sb("prob", [P, NP_, 512])
        probT = sb("probT", [P, NPT, 512])
        oT = sb("oT", [P, NJ, T])
        nmax = sb("nmax", [P, NS, 2])
        rsum = sb("rsum", [P, NS, 2])
        rinv = sb("rinv", [P, NS, 2])
        stats = sb("stats", [P, 2, NT, 6])
        mv = sb("mv", [P, 2, NT, 2])
        vareps = sb("vareps", [P, 2, NT])
        rstd = sb("rstd", [P, 2, NT])
        ident = sb("ident", [P, P])
        mask = sb("mask", [P, T])
        rope_q = sb("rope_q", [P, NJ, 2, TPH])
        cos_k = sb("cos_k", [P, HD // 2])
        sin_k = sb("sin_k", [P, HD // 2])
        bias = sb("bias", [P, C])
        alpha = sb("alpha", [P, 1])
        ones = sb("ones", [P, P])
        half_pow = sb("half_pow", [P, NT])
        thr = sb("thr", [P, 4])

        ps_s = [ctx.enter_context(nc.psum_tensor(f"ps_s{n}", [P, 512], F32)) for n in range(NS)]
        ps_t = [ctx.enter_context(nc.psum_tensor(f"ps_t{n}", [P, 512], F32)) for n in range(NPT)]
        ps_o = ctx.enter_context(nc.psum_tensor("ps_o", [P, 512], F32))
        ps_m = [ctx.enter_context(nc.psum_tensor(f"ps_m{n}", [P, 512], F32)) for n in range(2)]

        xn_dram = nc.dram_tensor("xn_dram", (B, P, NT * C), F32)

        x_loaded = [sem(f"x_loaded{n}") for n in range(2)]
        ident_loaded = sem("ident_loaded")
        w0_loaded = [sem(f"w0_loaded{n}") for n in range(3)]
        w1_loaded = sem("w1_loaded")
        wf_loaded = [sem(f"wf_loaded{n}") for n in range(2)]
        const_loaded = sem("const_loaded")
        mask_loaded = sem("mask_loaded")
        experts_loaded = sem("experts_loaded")
        zeroed = sem("zeroed")
        pool_zeroed = sem("pool_zeroed")
        w0_hi, w0_split = sem("w0_hi"), sem("w0_split")
        w1_hi, w1_split = sem("w1_hi"), sem("w1_split")
        thr_step, abs_sum, wf_split = sem("thr_step"), sem("abs_sum"), sem("wf_split")
        s_ready = sem("s_ready")
        max_ready = sem("max_ready")
        p_ready = sem("p_ready")
        rinv_ready = sem("rinv_ready")
        norm_ready = sem("norm_ready")
        t_ready = sem("t_ready")
        t_copied = [sem(f"t_copied{n}") for n in range(2)]
        pv_done = sem("pv_done")
        o_copied = sem("o_copied")
        m_ready = [sem(f"m_ready{n}") for n in range(2)]
        m_done = [sem(f"m_done{n}") for n in range(2)]
        xt_hi = [sem(f"xt_hi{n}") for n in range(2)]
        even_copied = sem("even_copied")
        k_rot = sem("k_rot")
        x1_step = sem("x1_step")
        ln_stat, ln_mv, ln_eps, ln_rstd, xn_ready = [[sem(f"{what}{n}") for n in range(2)] for what in (
            "ln_stat", "ln_mv", "ln_eps", "ln_rstd", "xn_ready")]
        xn_saved = sem("xn_saved")
        passed = sem("passed")
        xn_loaded = sem("xn_loaded")
        routing_loaded = sem("routing_loaded")
        route = sem("route")
        route_exp = sem("route_exp")
        disp_ready = sem("disp_ready")
        split_hi, split_lo = sem("split_hi"), sem("split_lo")
        h_ready, h_gelu = sem("h_ready"), sem("h_gelu")
        y_ready, y_copied = sem("y_ready"), sem("y_copied")
        ys_ready, ys_copied = sem("ys_ready"), sem("ys_copied")
        c_ready, out_ready = sem("c_ready"), sem("out_ready")
        out_stored = sem("out_stored")

        xn_all = v_col[:, :, :].rearrange("p n c -> p (n c)")
        w0_flat = w0[:, :, :, :].rearrange("p l a n -> p (l a n)")
        disp = w0_flat[:, 0:4096].rearrange("p (n s) -> p n s", n=B * NT)
        xn_hi, xn_lo = w0_flat[:, 4096:6144], wq1[:, 0, :]
        xe = xn_all.rearrange("p (e b s) -> p e b s", e=E, b=B)
        dT_part = wkv1[:, :, :, :].rearrange("p l a n -> p (l a n)").rearrange("p (b f) -> p b f", b=B)
        dT = dT_part.bitcast(F32)
        w1_sb = q_flat.rearrange("p (e f) -> p e f", e=E)
        w2_sb = k_flat.rearrange("p (e f d) -> p e f d", e=E, f=NF)
        yT = v_row[:, 0:E * B * CAP].rearrange("p (b e s) -> p b e s", b=B, e=E)
        ys = oT[:, :, :].rearrange("p j t -> p (j t)").rearrange("p (b g d) -> p b g d", b=B, g=2)
        ps_y = [ps_o, ps_t[0]]
        hid = [prob[:, 0:2, :].rearrange("p a f -> p (a f)"), probT[:, :, :].rearrange("p a f -> p (a f)")]
        upper = mem0[:, 8192:8320]
        iota = mem0[:, 8320:8576]
        first_slot = mem0[:, 8576:8704].rearrange("p (n e) -> p n e", e=E)
        rank = mem0[:, 8704:8832].rearrange("p (n e) -> p n e", e=E)
        wide = [x[:, n * 128:(n + 1) * 128].rearrange("p (n e) -> p n e", e=E) for x in (sin_k, cos_k) for n in range(4)]
        thin = [mask[:, n * 16:(n + 1) * 16] for n in range(10)]

        block = ctx.enter_context(nc.Block())

        def w1_part(n, low):
            half = slice(n % 2 * 512, (n % 2 + 1) * 512)
            return wq1[:, low, n * 512:(n + 1) * 512] if n < 4 else wkv1[:, low, n // 2 - 2, half]

        def turned_k(eng, kind, i, o, m, e, late):
            src = o[e * DK:(e + 1) * DK, :].rearrange("p (j h t) -> p j h t", j=2, h=H)
            for half in range(2):
                dst = (k_last if late else k_dup)[half * DK:(half + 1) * DK, :, e, 2 * m:2 * m + 2, :].rearrange("p h j t -> p j h t")
                if e == 0:
                    ins = eng.activation(dst, src, ACT.Copy)
                else:
                    if half:
                        n = order("kTz" if late else "kT", kind).index(m)
                        eng.wait_ge(even_copied, (i - 1 + late) * 4 + n + 1)
                    ins = eng.tensor_copy(dst, src)
            if e == 0:
                ins.then_inc(even_copied, 1)
            return ins

        def wait_apart(eng, s, value):
            eng.wait_ge(s, value)
            if not isinstance(value, int):
                eng.sem_inc(passed, 1)

        def ln_number(block_no, i):
            return i if block_no else i + 1

        @block.sync
        def _(sp):
            xv = t_in["x"].rearrange("b (t p) c -> p (b t) c", p=P)
            sp.dma_start(x_all[:, 0:NT, :], xv[:, 0:NT, :]).then_inc(x_loaded[0], 16)
            sp.dma_start(wf_raw[:, :], t_in["wf"]).then_inc(wf_loaded[0], 16)
            sp.dma_start(q_flat[:, 0:HD], t_in["w0"][:, 0:HD]).then_inc(w0_loaded[0], 16)
            sp.dma_start(ident[:, :], t_in["ident"]).then_inc(ident_loaded, 16)
            for n in (1, 2):
                sp.dma_start(q_flat[:, n * HD:(n + 1) * HD], t_in["w0"][:, n * HD:(n + 1) * HD]).then_inc(w0_loaded[n], 16)
            sp.dma_start(wg_raw[:, :], t_in["wg"]).then_inc(wf_loaded[1], 16)
            sp.dma_start(alpha[:, :], t_in["alpha"]).then_inc(wf_loaded[1], 16)
            sp.dma_start(mask[:, :], t_in["mask"]).then_inc(mask_loaded, 16)
            sp.dma_start(x_all[:, NT:, :], xv[:, NT:, :]).then_inc(x_loaded[1], 16)
            sp.dma_start(bias[:, :], t_in["bias"]).then_inc(const_loaded, 16)
            sp.dma_start(lin[:, :, :], t_in["lin"].rearrange("(j p) z -> p j z", p=P)).then_inc(const_loaded, 16)
            sp.dma_start(k_flat, t_in["w1"]).then_inc(w1_loaded, 16)
            sp.dma_start(wo[:, :, :], t_in["wo"].rearrange("(j p) z -> p j z", p=P)).then_inc(const_loaded, 16)
            sp.dma_start(rope_q[:, :, :, :].rearrange("p j a t -> p (j a t)"), t_in["rope_q"]).then_inc(const_loaded, 16)
            sp.dma_start(cos_k[:, :], t_in["cos_k"]).then_inc(const_loaded, 16)
            sp.dma_start(sin_k[:, :], t_in["sin_k"]).then_inc(const_loaded, 16)
            with sp.Fori(0, B) as i:
                sp.wait_ge(xn_ready[1], i + 1)
                sp.dma_start(xn_dram[bass.ds(i, 1), :, :].rearrange("b p f -> p (b f)"),
                             xn1[:, :, :].rearrange("p t c -> p (t c)")).then_inc(xn_saved, 16)
            sp.wait_ge(xn_saved, 16 * B)

            sp.wait_ge(k_rot, 4 * B)
            sp.dma_start(mem0[:, 8192:8192 + ROUTING], t_in["routing"]).then_inc(routing_loaded, 16)
            for n in range(4):
                bank, place = task_at(LAST, "vT", n)
                sp.wait_ge(m_ready[bank], task_base(I_LAST, bank) + place)
            sp.dma_start(xn_all.rearrange("p (b f) -> p b f", b=B), xn_dram[:, :, :].rearrange("b p f -> p b f")).then_inc(xn_loaded, 16)
            sp.wait_ge(s_ready, head_base(I_LAST))
            sp.dma_start(w1_sb, t_in["We1"].rearrange("e d f -> d e f")).then_inc(experts_loaded, 16)
            for e in range(E):
                sp.dma_start(w2_sb[:, e, :, :], t_in["We2"][e].rearrange("(f p) d -> p f d", p=P)).then_inc(experts_loaded, 16)
            ov = out.rearrange("b (t p) c -> p (b t) c", p=P)
            for b in range(B):
                sp.wait_ge(out_ready, b + 1)
                sp.dma_start(ov[:, b * NT:(b + 1) * NT, :], x_all[:, b * NT:(b + 1) * NT, :]).then_inc(out_stored, 16)
            sp.wait_ge(out_stored, 16 * B)

        @block.tensor
        def _(pe):
            def three(o, wh, wl, xh, xl, start=True, stop=True):
                pe.matmul(o, wh, xh, start=start, stop=False)
                pe.matmul(o, wh, xl, start=False, stop=False)
                return pe.matmul(o, wl, xh, start=False, stop=stop)

            def landed(kind, i, tasks, bank=None, place=0):
                most = {bank: place} if bank is not None else {}
                for name, n in tasks:
                    b, p = task_at(kind, name, n)
                    most[b] = max(most.get(b, 0), p)
                for b, p in sorted(most.items()):
                    if p or not (isinstance(i, int) and i == -1):
                        pe.wait_ge(m_done[b], task_base(i, b) + p)

            def task(kind, i, what, m, bank, place):
                o = ps_m[bank]
                reads = []
                if is_first(kind, ("q0", "k0", "v0"), what, m):
                    reads = [("xT0", 0)]
                elif is_first(kind, ("vT",), what, m) and kind != LAST:
                    reads = [("v1", n) for n in range(4)]
                elif is_first(kind, ("v1z", "k1z", "q1z"), what, m):
                    reads = [("xT1", 0)]
                elif what == "logit":
                    reads = [("xT1", 0)]
                landed(kind, i, reads, bank, place - 1)
                if kind == LAST and is_first(kind, ("vT",), what, m):
                    landed(NO_NEXT, I_NO_NEXT, [("v1z", n) for n in range(4)])
                late = what.endswith("z")
                what = what.rstrip("z")
                if kind == PRO and what in ("q0", "k0", "v0") and m == 0:
                    pe.wait_ge(w0_split, 1 + ("q0", "k0", "v0").index(what))
                if kind == FIRST and what == "proj0":
                    pe.wait_ge(thr_step, 2)
                    pe.wait_ge(const_loaded, 16 * N_CONST)
                if what == "xT0" or what == "xT1":
                    n = int(what == "xT1")
                    pe.wait_ge(xn_ready[n], ln_number(n, i) + 1)
                    src = xn1 if n else xn0
                    for t in range(NT):
                        last = pe.transpose(o[:, t * P:(t + 1) * P], src[:, t, :], ident[:, :])
                elif what in ("q0", "k0"):
                    w = 0 if what == "q0" else 1
                    for a in range(2):
                        col = slice((2 * m + a) * P, (2 * m + a + 1) * P)
                        last = three(o[:, a * T:(a + 1) * T], w0[:, 0, w, col], w0[:, 1, w, col],
                                     xT0[:, 0, :], xT0[:, 1, :])
                elif what == "v0":
                    t, f = m // 2, m % 2
                    tok, col = slice(t * P, (t + 1) * P), slice(f * 512, (f + 1) * 512)
                    last = three(o[:, :], xT0[:, 0, tok], xT0[:, 1, tok], w0[:, 0, 2, col], w0[:, 1, 2, col])
                elif what == "q1":
                    for a in range(2):
                        col = slice((2 * m + a) * P, (2 * m + a + 1) * P)
                        last = three(o[:, a * T:(a + 1) * T], wq1[:, 0, col], wq1[:, 1, col],
                                     xT1[:, 0, :], xT1[:, 1, :])
                elif what == "k1":
                    f, t = m // 2, m % 2
                    tok, col = slice(t * P, (t + 1) * P), slice(f * 512, (f + 1) * 512)
                    last = three(o[:, :], xT1[:, 0, tok], xT1[:, 1, tok], wkv1[:, 0, 0, col], wkv1[:, 1, 0, col])
                elif what == "v1":
                    for a in range(2):
                        col = slice((2 * m + a) * P, (2 * m + a + 1) * P)
                        last = three(o[:, a * T:(a + 1) * T], wkv1[:, 0, 1, col], wkv1[:, 1, 1, col],
                                     xT1[:, 0, :], xT1[:, 1, :])
                elif what == "kT":
                    pe.wait_ge(k_rot, (i - 1 + late) * 4 + 2 * (m // 2) + 2)
                    for a in range(2):
                        c = (2 * m + a) % 4
                        for t in range(NT):
                            src = k_tok[:, t, c * P:(c + 1) * P]
                            last = pe.transpose(o[:, a * T + t * P:a * T + (t + 1) * P], src, ident[:, :])
                elif what == "vT":
                    for a in range(4):
                        last = pe.transpose(o[:, a * P:(a + 1) * P], v_col[:, 4 * m + a, :], ident[:, :])
                elif what == "place":
                    pe.wait_ge(routing_loaded, 16)
                    pe.wait_ge(route, ROUTE_MASK)
                    chosen = wide[5].rearrange("p (b t) e -> p b t e", t=NT)
                    pe.matmul(o[:, 0:B * E], upper, chosen[:, :, 0, :], start=True, stop=True)
                    pe.matmul(o[:, B * E:2 * B * E], upper, chosen[:, :, 1, :], start=True, stop=False)
                    last = pe.matmul(o[:, B * E:2 * B * E], ones[:, :], chosen[:, :, 0, :], start=False, stop=True)
                elif what == "xe":
                    pe.wait_ge(disp_ready, 2 * m + 2)
                    pe.wait_ge(split_lo, 4)
                    for n in range(2 * NT * m, 2 * NT * (m + 1)):
                        half = slice(n // NT % 2 * T, (n // NT % 2 + 1) * T)
                        pe.matmul(o[:, half], xn_hi[:, n * C:(n + 1) * C], disp[:, n, :], start=(n % NT == 0), stop=False)
                        last = pe.matmul(o[:, half], xn_lo[:, n * C:(n + 1) * C], disp[:, n, :], start=False,
                                         stop=(n % NT == NT - 1))
                elif what == "dT":
                    pe.wait_ge(disp_ready, m + 1)
                    for g in range(2):
                        for t in range(NT):
                            last = pe.transpose(o[:, g * T + t * P:g * T + (t + 1) * P],
                                                disp[:, m * NT + t, g * P:(g + 1) * P].bitcast(F32), ident[:, :])
                elif what == "proj0" or what == "proj1":
                    n_pairs = NJ if what == "proj0" or kind == LAST else 2 * NJ
                    pe.wait_ge(o_copied, pair_base(i) + n_pairs)
                    w = lin if what == "proj0" else wo
                    for t in range(NT):
                        tok = slice(t * P, (t + 1) * P)
                        for j in range(NJ):
                            last = pe.matmul(o[:, tok], oT[:, j, tok], w[:, j, :], start=(j == 0),
                                             stop=(what == "proj1" and j == NJ - 1))
                        if what == "proj0":
                            if kind == FIRST:
                                pe.wait_ge(wf_split, 2)
                            last = three(o[:, tok], xT0[:, 0, tok], xT0[:, 1, tok], we[:, 0, :], we[:, 1, :],
                                         start=False)
                elif what == "logit":
                    for t in range(NT):
                        tok = slice(t * P, (t + 1) * P)
                        last = three(o[:, t * E:(t + 1) * E], xT1[:, 0, tok], xT1[:, 1, tok],
                                     wg[:, 0, :], wg[:, 1, :])
                last.then_inc(m_ready[bank], 1)

            def scores(kind, i, k):
                o = ps_s[k % NS]
                a = heads_a(kind)
                if k >= NS:
                    pe.wait_ge(p_ready, head_base(i) + k - NS + 1)
                if k < a:
                    j, hh = k // 2, k % 2
                    if k == 0:
                        for n in range(2):
                            after = [tasks_in(x, n) - max(p for what, _, b, p in schedule(x) if b == n and what in ("q0", "k0", "v0"))
                                     for x in ([PRO] if kind == FIRST else [FIRST, FULL])]
                            pe.wait_ge(m_done[n], task_base(i, n) - min(after))
                    pe.matmul(o[:, 0:P], q_pad[:, j, hh, 0:P], k_pair[:, j, 0:P], start=True, stop=True)
                    last = pe.matmul(o[:, P:P + T], q_pad[:, j, hh, P:T], k_pair[:, j, :], start=True, stop=True)
                else:
                    h = k - a
                    if h == 0 and kind == LAST:
                        landed(NO_NEXT, I_NO_NEXT, [t[1:] for t in NO_NEXT_TASKS if t[1] in ("q1z", "kTz")])
                    elif h == 0:
                        landed(kind, i, [t[1:] for t in QKV1 if t[1] in ("q1", "kT", "vT")])
                    q, kk = (q_last, k_last) if kind == LAST else (q_rot, k_dup)
                    for e in range(2):
                        last = pe.matmul(o[:, e * T:(e + 1) * T], q[:, h, e, :, :].rearrange("p j t -> p (j t)"),
                                         kk[:, h, :, :, :].rearrange("p a j t -> p (a j t)"), start=True, stop=True)
                last.then_inc(s_ready, 1)

            def transposes(kind, i, k):
                o, src = ps_t[k % NPT], prob[:, k % NP_, :]
                pe.wait_ge(norm_ready, head_base(i) + k + 1)
                if k >= NPT:
                    pe.wait_ge(t_copied[k % 2], pair_base(i) + k // 2)
                if k < heads_a(kind):
                    blocks = [(0, 0), (1, 1), (2, 2)]
                else:
                    blocks = [(0, 0), (1, 2), (2, 1), (3, 3)]
                for dst, s in blocks:
                    last = pe.transpose(o[:, dst * P:(dst + 1) * P], src[:, s * P:(s + 1) * P], ident[:, :])
                last.then_inc(t_ready, 1)

            def outputs(kind, i, k):
                a = heads_a(kind)
                pt = probT[:, k % NPT, :]
                pe.wait_ge(t_copied[k % 2], pair_base(i) + k // 2 + 1)
                pair = k // 2
                if kind == LAST and k == 0:
                    landed(kind, i, [("vT", n) for n in range(4)])
                if k % 2 == 0 and pair >= 1:
                    pe.wait_ge(o_copied, pair_base(i) + pair)
                o = ps_o[:, 0:T]
                if k < a:
                    j, hh = k // 2, k % 2
                    pe.matmul(o, v_pair[:, 0, j, hh:hh + 2, :].rearrange("p a d -> p (a d)"), pt[:, 0:T],
                              start=(hh == 0), stop=False)
                    last = pe.matmul(o[:, P:T], v_pair[:, 1, j, hh:hh + 2, :].rearrange("p a d -> p (a d)"), pt[:, T:384],
                                     start=False, stop=(hh == 1))
                else:
                    h = k - a
                    oh = o[:, (k % 2) * P:(k % 2 + 1) * P]
                    for kb in range(2):
                        at = P * (2 * h + kb)
                        for e in range(2):
                            w = v_row[:, at + 64:at + 64 + P] if e == 0 else v_row[:, at:at + P]
                            last = pe.matmul(oh, w, pt[:, (2 * kb + e) * P:(2 * kb + e + 1) * P],
                                             start=(kb == 0 and e == 0), stop=(kb == 1 and e == 1))
                last.then_inc(pv_done, 1)

            def iteration(kind, i):
                for what, m, bank, place in schedule(kind):
                    if what == "S":
                        scores(kind, i, m)
                    elif what == "T":
                        transposes(kind, i, m)
                    elif what == "PV":
                        outputs(kind, i, m)
                    elif what == "wf":
                        pe.wait_ge(thr_step, 1)
                        pe.wait_ge(zeroed, 4)
                        pe.wait_ge(m_done[0], tasks_in(PRO, 0))
                        pe.matmul(ps_m[0][:, 0:1], ones[:, :], thr[:, 0:1], start=True, stop=True).then_inc(abs_sum, 1)
                    elif bank is not None:
                        if kind == LAST and place == 1:
                            landed(kind, i, [], 1 - bank, 0)
                        task(kind, i, what, m, bank, place)

            pe.wait_ge(ident_loaded, 16)
            iteration(PRO, -1)
            pe.wait_ge(zeroed, 4)
            iteration(FIRST, 0)
            pe.wait_ge(w1_split, 8)
            with pe.Fori(I_LOOP, I_NO_NEXT) as i:
                iteration(FULL, i)
            iteration(NO_NEXT, I_NO_NEXT)
            iteration(LAST, I_LAST)

            pe.wait_ge(experts_loaded, 16 * (E + 1))
            for n in range(2):
                pe.wait_ge(t_copied[n], pair_base(I_LAST) + NJ)
                pe.wait_ge(m_done[n], task_base(I_LAST, n) + tasks_in(LAST, n))

            def hidden(e):
                for f2 in range(2):
                    n = 2 * e + f2
                    if n >= NS:
                        pe.wait_ge(h_gelu, n - NS + 1)
                    for f in range(2):
                        col = slice((2 * f2 + f) * P, (2 * f2 + f + 1) * P)
                        last = pe.matmul(ps_s[n % NS][:, f * T:(f + 1) * T], w1_sb[:, e, col],
                                         xe[:, e, :, :].rearrange("p b s -> p (b s)"), start=True, stop=True)
                    last.then_inc(h_ready, 1)

            hidden(0)
            for e in range(E):
                if e + 1 < E:
                    hidden(e + 1)
                pe.wait_ge(h_gelu, 2 * e + 2)
                if e >= 2:
                    pe.wait_ge(y_copied, e - 1)
                for f in range(NF):
                    last = pe.matmul(ps_y[e % 2][:, 0:T], w2_sb[:, e, f, :], hid[e % 2][:, f * T:(f + 1) * T],
                                     start=(f == 0), stop=(f == NF - 1))
                last.then_inc(y_ready, 1)
            pe.wait_ge(y_copied, E)

            def turn(n):
                if n >= 2:
                    pe.wait_ge(ys_copied, n - 1)
                for b in range(2):
                    for g in range(2):
                        last = pe.transpose(ps_t[n % 2][:, (2 * b + g) * P:(2 * b + g + 1) * P],
                                            yT[:, 2 * n + b, 4 * g:4 * g + 4, :].rearrange("p e s -> p (e s)"), ident[:, :])
                last.then_inc(ys_ready, 1)

            turn(0)
            for n in range(B // 2):
                if n + 1 < B // 2:
                    turn(n + 1)
                pe.wait_ge(ys_copied, n + 1)
                for b in (2 * n, 2 * n + 1):
                    if b >= 2:
                        pe.wait_ge(out_ready, b - 1)
                    for t in range(NT):
                        for g in range(2):
                            last = pe.matmul(ps_m[b % 2][:, t * P:(t + 1) * P], dT[:, b, g * T + t * P:g * T + (t + 1) * P],
                                             ys[:, b, g, :], start=(g == 0), stop=(g == 1))
                    last.then_inc(c_ready, 1)

        @block.vector
        def _(dve):
            def ln_stats(b, i):
                n = ln_number(b, i)
                rows = batch_rows(i if b else i + 1)
                dve.wait_ge(x_loaded[0 if isinstance(i, int) and i == -1 else 1], 16)
                if b:
                    wait_apart(dve, x1_step, i + 1)
                for t in range(NT):
                    dve.bn_stats(stats[:, b, t, :],
                                 x_all[:, bass.ds(rows + t, 1), :].rearrange("p a c -> p (a c)")).then_inc(ln_stat[b], 1)
                wait_apart(dve, ln_stat[b], n * NT + NT)
                for t in range(NT):
                    dve.bn_aggr(mv[:, b, t, :], stats[:, b, t, :]).then_inc(ln_mv[b], 1)

            def ln_apply(b, i):
                n = ln_number(b, i)
                rows = batch_rows(i if b else i + 1)
                dst = xn1 if b else xn0
                dve.wait_ge(ln_rstd[b], n + 1)
                if b and not (isinstance(i, int) and i == 0):
                    dve.wait_ge(xn_saved, i * 16)
                for t in range(NT):
                    ins = dve.tensor_scalar(dst[:, t, :], x_all[:, bass.ds(rows + t, 1), :].rearrange("p a c -> p (a c)"),
                                            mv[:, b, t, 0:1], rstd[:, b, t:t + 1], ALU.subtract, ALU.mult)
                ins.then_inc(xn_ready[b], 1)

            def task(kind, i, what, m, bank, place):
                if what in ("q0", "v1", "v1z", "vT", "xe") or (what == "dT" and m % 2):
                    return
                o = ps_m[bank]
                late = what.endswith("z")
                what = what.rstrip("z")
                dve.wait_ge(m_ready[bank], task_base(i, bank) + place)
                if kind == FIRST and what == "proj0":
                    dve.wait_ge(const_loaded, 16 * N_CONST)
                if what == "xT0" or what == "xT1":
                    n = int(what == "xT1")
                    dve.wait_ge(xt_hi[n], ln_number(n, i) + 1)
                    dst = xT0 if what == "xT0" else xT1
                    ins = dve.tensor_tensor(dst[:, 1, :], o[:, 0:T], dst[:, 0, :].bitcast(F32), ALU.subtract)
                elif what == "k0":
                    ins = dve.tensor_copy(k_pair[:, 2 * m:2 * m + 2, :].rearrange("p j t -> p (j t)"), o[:, :])
                elif what == "v0":
                    t, f = m // 2, m % 2
                    ins = dve.tensor_copy(v_pair[:, t, 4 * f:4 * f + 4, 0:3:2, :],
                                          o[:, :].rearrange("p (j a d) -> p j a d", j=4, a=2))
                elif what == "q1":
                    ins = dve.tensor_tensor((q_last if late else q_rot)[:, :, :, m, :].rearrange("p h a t -> p a h t"),
                                            o[:, :].rearrange("p (a h t) -> p a h t", a=2, h=H),
                                            rope_q[:, m, :, :].unsqueeze(2).broadcast_to([P, 2, H, TPH]), ALU.mult)
                elif what == "kT":
                    ins = turned_k(dve, kind, i, o, m, 1, late)
                elif what == "k1":
                    f, t = m // 2, m % 2
                    cos, sin = (k_cos_last, k_sin_last) if late else (k_cos, k_sin)
                    if m:
                        dve.wait_ge(k_rot, (i - 1 + late) * 4 + m)
                    dve.tensor_tensor(cos.rearrange("p (a b) -> p a b", b=2),
                                      o[:, :].rearrange("p (a b) -> p a b", b=2),
                                      cos_k[:, f * 256:(f + 1) * 256].unsqueeze(2).broadcast_to([P, 256, 2]), ALU.mult)
                    s = sin_k[:, f * 256:(f + 1) * 256]
                    d = sin.rearrange("p (a b) -> p a b", b=2)
                    ov = o[:, :].rearrange("p (a b) -> p a b", b=2)
                    dve.scalar_tensor_tensor(d[:, :, 0], ov[:, :, 1], -1.0, s, ALU.mult, ALU.mult)
                    ins = dve.tensor_tensor(d[:, :, 1], ov[:, :, 0], s, ALU.mult)
                elif what == "proj0":
                    rows = x_all[:, bass.ds(batch_rows(i), NT), :]
                    ins = dve.tensor_tensor(rows, o[:, 0:NT * C].rearrange("p (t c) -> p t c", t=NT), rows, ALU.add)
                    ins.then_inc(m_done[bank], 1)
                    dve.wait_ge(m_done[bank], task_base(i, bank) + place)
                    ins = dve.tensor_tensor(rows, rows, bias[:, :].unsqueeze(1).broadcast_to([P, NT, C]), ALU.add)
                    ins.then_inc(x1_step, 1)
                    return
                elif what == "proj1":
                    rows = x_all[:, bass.ds(batch_rows(i - 1), NT), :]
                    ins = dve.tensor_tensor(rows, o[:, 0:NT * C].rearrange("p (t c) -> p t c", t=NT), rows, ALU.add)
                elif what == "place":
                    ins = dve.tensor_tensor(wide[6].rearrange("p (b t) e -> p t b e", t=NT),
                                            o[:, 0:2 * B * E].rearrange("p (t b e) -> p t b e", t=NT, b=B),
                                            wide[5].rearrange("p (b t) e -> p t b e", t=NT), ALU.mult)
                    ins.then_inc(m_done[bank], 1)
                    dve.wait_ge(m_done[bank], task_base(i, bank) + place)
                    return
                elif what == "dT":
                    ins = dve.tensor_copy(dT_part[:, m, :], o[:, :])
                elif what == "logit":
                    ins = dve.tensor_copy(lg_all[:, bass.ds(batch_rows(i), NT), :],
                                          o[:, 0:NT * E].rearrange("p (t e) -> p t e", t=NT))
                ins.then_inc(m_done[bank], 1)

            def ternary_weight():
                dve.wait_ge(wf_loaded[1], 32)
                dve.wait_ge(abs_sum, 1)
                dve.tensor_scalar(thr[:, 1:2], ps_m[0][:, 0:1], THRESH / (C * C), None, ALU.mult).then_inc(thr_step, 1)
                dve.wait_ge(thr_step, 2)
                dve.tensor_scalar(thr[:, 2:3], thr[:, 1:2], -1.0, None, ALU.mult).then_inc(thr_step, 1)
                dve.tensor_scalar(wf_above, wf_raw, thr[:, 1:2], None, ALU.is_gt).then_inc(thr_step, 1)
                dve.wait_ge(thr_step, 4)
                dve.scalar_tensor_tensor(we_sign, wf_raw, thr[:, 2:3], wf_above, ALU.is_lt, ALU.subtract).then_inc(thr_step, 1)
                dve.wait_ge(thr_step, 5)
                dve.tensor_scalar(we_full, we_sign, alpha[:, 0:1], -1.0, ALU.mult, ALU.mult).then_inc(thr_step, 1)
                dve.wait_ge(thr_step, 6)
                dve.tensor_copy(we[:, 0, :], we_full).then_inc(thr_step, 1)
                dve.tensor_copy(wg[:, 0, :], wg_raw).then_inc(thr_step, 1)
                dve.wait_ge(thr_step, 8)
                dve.tensor_tensor(we[:, 1, :], we_full, we[:, 0, :].bitcast(F32), ALU.subtract).then_inc(wf_split, 1)
                dve.tensor_tensor(wg[:, 1, :], wg_raw, wg[:, 0, :].bitcast(F32), ALU.subtract).then_inc(wf_split, 1)

            steps = [0]

            def then(ins):
                steps[0] += 1
                ins.then_inc(route, 1)
                dve.wait_ge(route, steps[0])

            def wider(a):
                return a.unsqueeze(2).broadcast_to([P, B * NT, E])

            top, total, inv, gate, best, pos, off, keep, slot = thin[0:9]

            def routing(part):
                logits = lg_all[:, :, :]
                if part == 0:
                    then(dve.tensor_reduce(top, logits, AX.X, ALU.max))
                    then(dve.tensor_tensor(wide[0], logits, wider(top), ALU.subtract))
                elif part == 1:
                    dve.wait_ge(route_exp, 1)
                    then(dve.tensor_reduce(total, wide[1], AX.X, ALU.add))
                    then(dve.reciprocal(inv, total))
                    then(dve.tensor_tensor(wide[2], wide[1], wider(inv), ALU.mult))
                    then(dve.tensor_reduce(gate, wide[2], AX.X, ALU.max))
                elif part == 2:
                    dve.wait_ge(routing_loaded, 16)
                    then(dve.tensor_tensor(wide[3], wide[2], wider(gate), ALU.is_equal))
                    then(dve.tensor_tensor(wide[4], wide[3], rank, ALU.mult))
                    then(dve.tensor_reduce(best, wide[4], AX.X, ALU.max))
                    then(dve.tensor_tensor(wide[5], wide[4], wider(best), ALU.is_equal))
                    assert steps[0] == ROUTE_MASK
                    then(dve.tensor_tensor(wide[7], wide[5], first_slot, ALU.mult))
                    then(dve.tensor_reduce(off, wide[7], AX.X, ALU.add))
                elif part == 3:
                    then(dve.tensor_reduce(pos, wide[6], AX.X, ALU.add))
                    then(dve.tensor_scalar(keep, pos, float(CAP), None, ALU.is_lt))
                    then(dve.tensor_tensor(slot, pos, off, ALU.add))
                    then(dve.scalar_tensor_tensor(slot, slot, 1.0, keep, ALU.add, ALU.mult))
                    then(dve.tensor_scalar(slot, slot, -1.0, None, ALU.add))

            def maxima(kind, i, k):
                o, nm = ps_s[k % NS], nmax[:, k % NS, :]
                if kind == FIRST and k == 0:
                    dve.wait_ge(mask_loaded, 16)
                wait_apart(dve, s_ready, head_base(i) + k + 1)
                if k < heads_a(kind):
                    dve.tensor_tensor_reduce(o[:, 0:P], o[:, 0:P], mask[:, P:T], -1.0, BIG, ALU.add, ALU.min, nm[:, 0:1])
                    ins = dve.tensor_tensor_reduce(o[:, P:384], o[:, P:384], mask[:, :], -1.0, BIG, ALU.add,
                                                   ALU.min, nm[:, 1:2])
                else:
                    ins = dve.tensor_reduce(nm, o[:, :].rearrange("p (a t) -> p a t", a=2), AX.X, ALU.max, negate=True)
                ins.then_inc(max_ready, 1)

            def iteration(kind, i):
                for what, m, bank, place in schedule(kind):
                    if what == "S":
                        maxima(kind, i, m)
                    elif what == "R":
                        dve.wait_ge(p_ready, head_base(i) + m + 1)
                        dve.reciprocal(rinv[:, m % NS, :], rsum[:, m % NS, :]).then_inc(rinv_ready, 1)
                    elif what == "T" and m % 2 == 1:
                        dve.wait_ge(t_ready, head_base(i) + m + 1)
                        if m >= NPT:
                            dve.wait_ge(pv_done, head_base(i) + m - NPT + 1)
                        n = 384 if m < heads_a(kind) else 512
                        dve.tensor_copy(probT[:, m % NPT, 0:n], ps_t[m % NPT][:, 0:n]).then_inc(t_copied[1], 1)
                    elif what == "stat":
                        ln_stats(m, i)
                    elif what == "norm":
                        ln_apply(m, i)
                    elif what == "route":
                        routing(m)
                    elif what == "split":
                        part = slice(m * 512, (m + 1) * 512)
                        dve.wait_ge(split_hi, m + 1)
                        dve.tensor_tensor(xn_lo[:, part], xn_all[:, part], xn_hi[:, part].bitcast(F32),
                                          ALU.subtract).then_inc(split_lo, 1)
                    elif what == "slots":
                        for n in range(m * NT, (m + 1) * NT):
                            ins = dve.tensor_scalar(disp[:, n, :], iota, slot[:, n:n + 1], None, ALU.is_equal)
                        ins.then_inc(disp_ready, 1)
                    elif what == "zeros":
                        dve.memset(ones[:, :], 1.0).then_inc(zeroed, 1)
                        dve.memset(v_pair[:, :, :, 1, :], 0.0).then_inc(zeroed, 1)
                    elif what == "wf":
                        ternary_weight()
                    elif what == "w0":
                        dve.wait_ge(w0_hi, m + 1)
                        dve.tensor_tensor(w0[:, 1, m, :], q_flat[:, m * HD:(m + 1) * HD], w0[:, 0, m, :].bitcast(F32),
                                          ALU.subtract).then_inc(w0_split, 1)
                    elif what == "w1lo":
                        dve.wait_ge(w1_hi, m + 1)
                        dve.tensor_tensor(w1_part(m, 1), k_flat[:, m * 512:(m + 1) * 512], w1_part(m, 0).bitcast(F32),
                                          ALU.subtract).then_inc(w1_split, 1)
                    elif bank is not None:
                        task(kind, i, what, m, bank, place)

            dve.memset(half_pow[:, :], -0.5).then_inc(zeroed, 1)
            dve.memset(q_pad[0:DK, :, 1, :], 0.0).then_inc(zeroed, 1)
            dve.wait_ge(wf_loaded[0], 16)
            dve.tensor_reduce(thr[:, 0:1], wf_raw, AX.X, ALU.add, apply_absolute_value=True).then_inc(thr_step, 1)
            iteration(PRO, -1)
            iteration(FIRST, 0)
            with dve.Fori(I_LOOP, I_NO_NEXT) as i:
                iteration(FULL, i)
            iteration(NO_NEXT, I_NO_NEXT)
            iteration(LAST, I_LAST)

            for e in range(E):
                dve.wait_ge(y_ready, e + 1)
                dve.tensor_copy(yT[:, :, e, :], ps_y[e % 2][:, 0:T].rearrange("p (b s) -> p b s", b=B)).then_inc(y_copied, 1)
            for b in range(B):
                dve.wait_ge(c_ready, b + 1)
                for t in range(NT):
                    n = b * NT + t
                    ins = dve.scalar_tensor_tensor(x_all[:, n, :], ps_m[b % 2][:, t * P:(t + 1) * P], gate[:, n:n + 1],
                                                   x_all[:, n, :], ALU.mult, ALU.add)
                ins.then_inc(out_ready, 1)

        @block.scalar
        def _(act):
            def task(kind, i, what, m, bank, place):
                o = ps_m[bank]
                late = what.endswith("z")
                what = what.rstrip("z")
                if what not in ("xT0", "xT1", "q0", "kT", "v1", "vT", "xe") and not (what == "dT" and m % 2):
                    return
                act.wait_ge(m_ready[bank], task_base(i, bank) + place)
                if what == "xT0" or what == "xT1":
                    dst = xT0 if what == "xT0" else xT1
                    act.activation(dst[:, 0, :], o[:, 0:T], ACT.Copy).then_inc(xt_hi[int(what == "xT1")], 1)
                    return
                if what == "q0":
                    if kind == PRO and m == 0:
                        act.wait_ge(zeroed, 2)
                        act.wait_ge(pool_zeroed, 1)
                    for hh in range(2):
                        rows = slice(hh * DK, (hh + 1) * DK)
                        ins = act.activation(q_pad[rows, 2 * m:2 * m + 2, hh, :],
                                             o[rows, :].rearrange("p (j t) -> p j t", j=2), ACT.Copy, scale=float(DK) ** 0.5)
                elif what == "kT":
                    turned_k(act, kind, i, o, m, 0, late)
                    return
                elif what == "dT":
                    ins = act.activation(dT_part[:, m, :], o[:, :], ACT.Copy)
                elif what == "xe":
                    ins = act.activation(xe[:, :, 2 * m:2 * m + 2, :].rearrange("p e b s -> p b e s"),
                                         o[:, :].rearrange("p (b e s) -> p b e s", b=2, e=E), ACT.Copy)
                elif what == "v1":
                    ins = act.activation(v_col[:, :, 2 * m * TPH:(2 * m + 2) * TPH].rearrange("p h (j t) -> p j h t", j=2),
                                         o[:, :].rearrange("p (j h t) -> p j h t", j=2, h=H), ACT.Copy)
                elif what == "vT":
                    if is_first(kind, ("vT",), what, m):
                        act.wait_ge(pool_zeroed, 2)
                    ins = act.activation(v_row[:, 64 + 8 * P * m:64 + 8 * P * (m + 1)].rearrange("p (a d) -> p a d", d=P)[:, :, 0:DK],
                                         o[:, :].rearrange("p (a d) -> p a d", d=DK), ACT.Copy)
                ins.then_inc(m_done[bank], 1)

            def exps(kind, i, k):
                o, nm, rs = ps_s[k % NS], nmax[:, k % NS, :], rsum[:, k % NS, :]
                p = prob[:, k % NP_, :]
                act.wait_ge(max_ready, head_base(i) + k + 1)
                if k >= NP_:
                    act.wait_ge(t_ready, head_base(i) + k - NP_ + 1)
                if k < heads_a(kind):
                    parts, scale = [(0, P), (P, 384)], -1.0
                else:
                    parts, scale = [(0, T), (T, 2 * T)], 1.0
                for n, (lo, hi) in enumerate(parts):
                    ins = act.activation(p[:, lo:hi], o[:, lo:hi], ACT.Exp, bias=nm[:, n:n + 1], scale=scale,
                                         accum_out=rs[:, n:n + 1])
                ins.then_inc(p_ready, 1)

            def iteration(kind, i):
                for what, m, bank, place in schedule(kind):
                    if what == "S":
                        exps(kind, i, m)
                    elif what == "T" and m % 2 == 0:
                        act.wait_ge(t_ready, head_base(i) + m + 1)
                        if m >= NPT:
                            act.wait_ge(pv_done, head_base(i) + m - NPT + 1)
                        n = 384 if m < heads_a(kind) else 512
                        act.activation(probT[:, m % NPT, 0:n], ps_t[m % NPT][:, 0:n], ACT.Copy).then_inc(t_copied[0], 1)
                    elif what == "route" and m == 0:
                        act.wait_ge(route, 2)
                        act.activation(wide[1], wide[0], ACT.Exp).then_inc(route_exp, 1)
                    elif what == "split":
                        act.wait_ge(xn_loaded, 16)
                        part = slice(m * 512, (m + 1) * 512)
                        act.activation(xn_hi[:, part], xn_all[:, part], ACT.Copy).then_inc(split_hi, 1)
                    elif what == "w0":
                        act.wait_ge(w0_loaded[m], 16)
                        act.activation(w0[:, 0, m, :], q_flat[:, m * HD:(m + 1) * HD], ACT.Copy).then_inc(w0_hi, 1)
                    elif what == "w1hi":
                        act.wait_ge(w1_loaded, 16)
                        act.activation(w1_part(m, 0), k_flat[:, m * 512:(m + 1) * 512], ACT.Copy).then_inc(w1_hi, 1)
                    elif what == "O":
                        act.wait_ge(pv_done, head_base(i) + 2 * m + 2)
                        src, p2 = ps_o[:, 0:T], m % NJ
                        if 2 * m < heads_a(kind):
                            ins = act.activation(oT[:, p2, :], src, ACT.Copy)
                        else:
                            ins = act.activation(oT[:, :, 2 * p2 * TPH:(2 * p2 + 2) * TPH].rearrange("p j (h t) -> p h j t", h=2),
                                                 src.rearrange("p (h j t) -> p h j t", h=2, j=NJ), ACT.Copy)
                        ins.then_inc(o_copied, 1)
                    elif bank is not None:
                        task(kind, i, what, m, bank, place)

            iteration(PRO, -1)
            iteration(FIRST, 0)
            with act.Fori(I_LOOP, I_NO_NEXT) as i:
                iteration(FULL, i)
            iteration(NO_NEXT, I_NO_NEXT)
            iteration(LAST, I_LAST)

            for n in range(2 * E):
                act.wait_ge(h_ready, n + 1)
                e, f2 = n // 2, n % 2
                if e >= 2:
                    act.wait_ge(y_ready, e - 1)
                act.activation(hid[e % 2][:, f2 * 512:(f2 + 1) * 512], ps_s[n % NS][:, :], ACT.Gelu_apprx_tanh).then_inc(h_gelu, 1)
            for n in range(B // 2):
                act.wait_ge(ys_ready, n + 1)
                act.activation(ys[:, 2 * n:2 * n + 2, :, :].rearrange("p b g d -> p (b g d)"), ps_t[n % 2][:, :],
                               ACT.Copy).then_inc(ys_copied, 1)

        @block.gpsimd
        def _(pool):
            def iteration(kind, i):
                for what, m, bank, place in schedule(kind):
                    if what == "R":
                        p, r = prob[:, m % NP_, :], rinv[:, m % NS, :]
                        pool.wait_ge(rinv_ready, head_base(i) + m + 1)
                        if m < heads_a(kind):
                            pool.tensor_tensor(p[:, 0:P], p[:, 0:P], r[:, 0:1].broadcast_to([P, P]), ALU.mult)
                            ins = pool.tensor_tensor(p[:, P:384], p[:, P:384], r[:, 1:2].broadcast_to([P, T]), ALU.mult)
                        else:
                            pv = p.rearrange("p (a t) -> p a t", a=2)
                            ins = pool.tensor_tensor(pv, pv, r.unsqueeze(2).broadcast_to([P, 2, T]), ALU.mult)
                        ins.then_inc(norm_ready, 1)
                    elif what == "stat":
                        n = ln_number(m, i)
                        wait_apart(pool, ln_mv[m], n * NT + NT)
                        pool.tensor_scalar(vareps[:, m, :], mv[:, m, :, 1], EPS, None, ALU.add).then_inc(ln_eps[m], 1)
                        pool.wait_ge(ln_eps[m], n + 1)
                        pool.tensor_tensor(rstd[:, m, :], vareps[:, m, :], half_pow[:, :], ALU.pow).then_inc(ln_rstd[m], 1)
                    elif what in ("k1", "k1z"):
                        t = m % 2
                        pool.wait_ge(m_done[bank], task_base(i, bank) + place)
                        terms = (k_cos, k_sin) if what == "k1" else (k_cos_last, k_sin_last)
                        pool.tensor_tensor(k_tok[:, t, :], *terms, ALU.add).then_inc(k_rot, 1)

            pool.wait_ge(zeroed, 1)
            iteration(PRO, -1)
            pool.wait_ge(ln_rstd[0], 1)
            pool.memset(q_pad[DK:P, :, 0, :], 0.0).then_inc(pool_zeroed, 1)
            pool.wait_ge(pool_zeroed, 1)
            pool.memset(v_row[:, :], 0.0).then_inc(pool_zeroed, 1)
            iteration(FIRST, 0)
            with pool.Fori(I_LOOP, I_NO_NEXT) as i:
                iteration(FULL, i)
            iteration(NO_NEXT, I_NO_NEXT)
            iteration(LAST, I_LAST)


_INS = ["x", "w0", "w1", "wf", "wg", "alpha", "bias", "lin", "wo", "We1", "We2",
        "ident", "mask", "rope_q", "cos_k", "sin_k", "routing"]


def constants():
    inv = 1.0 / 10000.0 ** (np.arange(0, DK, 2, dtype=np.float32) / DK)
    ang = np.outer(np.arange(T, dtype=np.float32), inv.astype(np.float32))
    cos = np.ones((T, DK // 2), np.float32)
    sin = np.zeros((T, DK // 2), np.float32)
    cos[1:], sin[1:] = np.cos(ang[:T - 1]), np.sin(ang[:T - 1])
    pos = np.arange(T).reshape(TPH, H)
    signed = np.stack([-sin, sin], -1).reshape(T, DK)
    both = np.concatenate([np.repeat(cos, 2, 1), signed], 1) / np.float32(DK ** 0.5)
    rope_q = both[pos.T.reshape(NJ, 2, TPH)].transpose(3, 0, 1, 2).reshape(P, T)
    rows = pos[np.arange(P) % TPH]
    cos_k, sin_k = cos[rows].reshape(P, HD // 2), sin[rows].reshape(P, HD // 2)
    q, k = np.arange(P)[:, None], np.arange(T)[None, :]
    mask = np.where(k > q + P, NEG, 0)
    upper = (np.arange(P)[:, None] < np.arange(P)[None, :])
    iota = np.tile(np.arange(E * CAP), (P, 1))
    first = np.tile(np.arange(E) * CAP, (P, B * NT))
    rank = np.tile(E - np.arange(E), (P, B * NT))
    routing = np.concatenate([upper, iota, first, rank], 1)
    return {n: np.ascontiguousarray(a, np.float32) for n, a in dict(
        ident=np.eye(P), mask=mask, rope_q=rope_q, cos_k=cos_k, sin_k=sin_k, routing=routing).items()}


def laid_out(a):
    rows = lambda w: np.asarray(w).reshape(C, HD)
    cols = lambda w: np.asarray(w).T
    q1 = cols(a["L1_attn_wq"]).reshape(C, H, 1, DK // 2, 2)
    q1 = np.concatenate([q1, q1[..., ::-1]], 2).reshape(C, 2 * HD)
    d = dict(
        x=a["L0_attn_x"],
        w0=np.concatenate([rows(a["L0_attn_query_mat"]), rows(a["L0_attn_key_mat"]), rows(a["L0_attn_value_mat"])], 1),
        w1=np.concatenate([q1, cols(a["L1_attn_wk"]), cols(a["L1_attn_wv"])], 1),
        wf=cols(a["L0_ffn_weight"]), wg=a["L1_ffn_Wg"],
        alpha=np.broadcast_to(np.asarray(a["L0_ffn_alpha"]), (P, 1)),
        bias=np.broadcast_to(np.asarray(a["L0_ffn_bias"]), (P, C)),
        lin=a["L0_attn_linear_m1"], wo=cols(a["L1_attn_wo"]), We1=a["L1_ffn_W1"], We2=a["L1_ffn_W2"])
    d.update(constants())
    return {n: np.ascontiguousarray(d[n]) for n in _INS}


def kernel(**inputs):
    import concourse.bacc as bacc
    from concourse.bass_utils import run_bass_kernel_spmd as run

    nc = bacc.Bacc("TRN2", target_bir_lowering=False, num_devices=1)
    arrays, aps = {}, {}
    for name, a in laid_out(inputs).items():
        arrays[f"in_{name}_dram"] = a
        aps[name] = nc.dram_tensor(f"in_{name}_dram", a.shape, mybir.dt.from_np(a.dtype), kind="ExternalInput").ap()
    out = nc.dram_tensor("out_0_dram", (B, T, C), F32, kind="ExternalOutput").ap()
    build(nc, aps, out)
    r = run(nc, [arrays], core_ids=[0])
    return r.results[0]["out_0_dram"]
```
